# Optimizing a Trainium2 kernel written in Bass

```python
import numpy as np
import jax
import jax.numpy as jnp

def _softmax(x, axis=-1):
    return jax.nn.softmax(x, axis=axis)

def _gelu(x):
    return jax.nn.gelu(x, approximate=True)

def _silu(x):
    return jax.nn.silu(x)

def _sigmoid(x):
    return jax.nn.sigmoid(x)

def _layernorm(x, axis=-1, eps=1e-05):
    m = jnp.mean(x, axis=axis, keepdims=True)
    v = jnp.var(x, axis=axis, keepdims=True)
    return (x - m) / jnp.sqrt(v + eps)

def _scatter_add(tgt, idx, src, axis=0):
    return tgt.at[idx].add(src)

def _segment_sum(src, seg, n):
    return jax.ops.segment_sum(src, seg, n)
kernel_name = 'mk_flamingo_gated_d2_seqx_r8_14a15c'

def setup_inputs(seed: int=0):
    np.random.seed(seed)
    _w = jnp.asarray

    def _rec_inputs():
        import jax
        import jax.numpy as jnp
        _rk = jax.random.key(seed)
        x = 7.22e-05 + 1 * jax.random.normal(jax.random.fold_in(_rk, 1), (128, 64, 128), jnp.float32)
        _lenS = 64 - jax.random.randint(jax.random.fold_in(_rk, 7), (128,), 0, max(1, 64 // 4) + 1, jnp.int32)
        _lenS2 = 64 - jax.random.randint(jax.random.fold_in(_rk, 8), (128,), 0, max(1, 64 // 4) + 1, jnp.int32)
        _ctx_1024P = jax.random.normal(jax.random.fold_in(_rk, 11), (128, 16, 128), jnp.float32)
        _ctx_1024c = jax.random.dirichlet(jax.random.fold_in(_rk, 511), 0.3 * jnp.ones((16,), jnp.float32), (128, 64))
        _ctx_1024t = jnp.einsum('bsk,bkd->bsd', _ctx_1024c, _ctx_1024P)
        _ctx_1024t = _ctx_1024t * jax.lax.rsqrt(jnp.mean(jnp.square(_ctx_1024t)) + 1e-12) * 0.953939
        ctx_1024 = 4.13588e-05 + 0.999923 * (_ctx_1024t + 0.3 * jax.random.normal(jax.random.fold_in(_rk, 611), (128, 64, 128), jnp.float32))
        _validS = jnp.arange(64)[None, :] < _lenS[:, None]
        _validS2 = jnp.arange(64)[None, :] < _lenS2[:, None]
        _causal = jnp.tril(jnp.ones((64, 64), dtype=bool))
        mask_BxS2_bf1 = jnp.ones((128, 64), dtype=bool)
        _g = jax.random.normal(jax.random.fold_in(_rk, 9001), (2, 2), jnp.float32)
        _g = jnp.sign(_g) * jnp.maximum(jnp.abs(_g), 1.0) + (_g == 0) * 1.0
        g_xattn = _g[0]
        g_ffn = _g[1]
        return (x, ctx_1024, mask_BxS2_bf1, g_xattn, g_ffn)
    x, ctx_1024, mask_BxS2_bf1, g_xattn, g_ffn = _rec_inputs()

    def _L0_xattn_setup():
        import jax, jax.numpy as jnp
        import numpy as np
        import math
        D_MODEL = 128
        N_HEADS = 16
        key = jax.random.key(seed)
        ks = jax.random.split(key, 11)
        B, T, D = (4, 256, D_MODEL)
        s = 1.0 / math.sqrt(D)
        inp = {'q': jax.random.normal(ks[0], (B, T, D), jnp.float32), 'k': jax.random.normal(ks[1], (B, T, D), jnp.float32), 'v': jax.random.normal(ks[2], (B, T, D), jnp.float32), 'wq': jax.random.normal(ks[3], (D, D), jnp.float32) * s, 'bq': jnp.zeros((D,), jnp.float32), 'wk': jax.random.normal(ks[4], (D, D), jnp.float32) * s, 'bk': jnp.zeros((D,), jnp.float32), 'wv': jax.random.normal(ks[5], (D, D), jnp.float32) * s, 'bv': jnp.zeros((D,), jnp.float32), 'wo': jax.random.normal(ks[6], (D, D), jnp.float32) * s, 'bo': jnp.zeros((D,), jnp.float32)}
        return inp
    _L0_xattn_all = _L0_xattn_setup()
    _L0_xattn_in = {k: v for k, v in _L0_xattn_all.items() if k in ('wq', 'bq', 'wk', 'bk', 'wv', 'bv', 'wo', 'bo')}
    del _L0_xattn_all

    def _L0_ffn_setup():
        import jax, jax.numpy as jnp
        import numpy as np
        B, S, H = (2, 256, 128)
        E, I, K = (8, 512, 2)

        def _moe_forward(x, gate_w, wg, wu, wd):
            b, s, h = x.shape
            x_flat = x.reshape(-1, h)
            logits = x_flat @ gate_w.T
            top_v, top_i = jax.lax.top_k(logits, K)
            probs = jax.nn.softmax(top_v.astype(jnp.float32), axis=-1).astype(logits.dtype)
            one_hot = jax.nn.one_hot(top_i, E, dtype=probs.dtype)
            combine = jnp.einsum('tk,tke->et', probs, one_hot)

            def body(acc, ws):
                wge, wue, wde, we = ws
                hidden = jax.nn.silu(x_flat @ wge.T) * (x_flat @ wue.T)
                return (acc + we[:, None] * (hidden @ wde.T), None)
            out, _ = jax.lax.scan(body, jnp.zeros_like(x_flat), (wg, wu, wd, combine))
            return out.reshape(b, s, h)
        key = jax.random.key(seed)
        ks = jax.random.split(key, 5)
        scale_h = 1.0 / np.sqrt(H)
        scale_i = 1.0 / np.sqrt(I)
        x = jax.random.normal(ks[0], (B, S, H), dtype=jnp.float32)
        gate_w = jax.random.normal(ks[1], (E, H), dtype=jnp.float32) * scale_h
        wg = jax.random.normal(ks[2], (E, I, H), dtype=jnp.float32) * scale_h
        wu = jax.random.normal(ks[3], (E, I, H), dtype=jnp.float32) * scale_h
        wd = jax.random.normal(ks[4], (E, H, I), dtype=jnp.float32) * scale_i
        return {'x': x, 'gate_w': gate_w, 'wg': wg, 'wu': wu, 'wd': wd}
    _L0_ffn_all = _L0_ffn_setup()
    _L0_ffn_in = {k: v for k, v in _L0_ffn_all.items() if k in ('gate_w', 'wg', 'wu', 'wd')}
    del _L0_ffn_all

    def _L1_xattn_setup():
        import jax, jax.numpy as jnp
        import numpy as np
        DIM = 128
        DIM_LATENT = 128
        DIM_HEAD = 64
        HEADS = 16
        INNER = HEADS * DIM_HEAD

        def layernorm(x, g, b, eps=1e-05):
            m = jnp.mean(x, axis=-1, keepdims=True)
            v = jnp.mean((x - m) ** 2, axis=-1, keepdims=True)
            return (x - m) / jnp.sqrt(v + eps) * g + b

        def rmsnorm(x, gamma, eps=1e-08):
            n = jnp.linalg.norm(x, axis=-1, keepdims=True) * x.shape[-1] ** (-0.5)
            return x / jnp.maximum(n, eps) * gamma
        key = jax.random.key(seed)
        ks = jax.random.split(key, 8)
        b, n, m = (4, 512, 64)
        x = jax.random.normal(ks[0], (b, n, DIM), dtype=jnp.float32)
        latents = jax.random.normal(ks[1], (b, m, DIM_LATENT), dtype=jnp.float32)
        mask = jnp.ones((b, n), dtype=bool)
        s = 0.02
        return {'x': x, 'latents': latents, 'mask': mask, 'ln_x_g': jnp.ones((DIM,), jnp.float32), 'ln_x_b': jnp.zeros((DIM,), jnp.float32), 'ln_l_g': jnp.ones((DIM_LATENT,), jnp.float32), 'ln_l_b': jnp.zeros((DIM_LATENT,), jnp.float32), 'qn_g': jnp.ones((DIM_HEAD,), jnp.float32), 'kn_g': jnp.ones((DIM_HEAD,), jnp.float32), 'Wq': jax.random.normal(ks[2], (DIM_LATENT, INNER), jnp.float32) * s, 'Wkv': jax.random.normal(ks[3], (DIM, 2 * INNER), jnp.float32) * s, 'Wout': jax.random.normal(ks[4], (INNER, DIM_LATENT), jnp.float32) * s, 'bout': jnp.zeros((DIM_LATENT,), jnp.float32)}
    _L1_xattn_all = _L1_xattn_setup()
    _L1_xattn_in = {k: v for k, v in _L1_xattn_all.items() if k in ('ln_x_g', 'ln_x_b', 'ln_l_g', 'ln_l_b', 'qn_g', 'kn_g', 'Wq', 'Wkv', 'Wout', 'bout')}
    del _L1_xattn_all

    def _L1_ffn_setup():
        import jax, jax.numpy as jnp
        import numpy as np
        HIDDEN = 128
        INNER = 512

        def _weight_quant(w):
            scale = 1.0 / jnp.clip(jnp.mean(jnp.abs(w)), 1e-05)
            wq = jnp.clip(jnp.round(w * scale), -1.0, 1.0) / scale
            return w + jax.lax.stop_gradient(wq - w)

        def _act_quant(x):
            scale = 127.0 / jnp.clip(jnp.max(jnp.abs(x), axis=-1, keepdims=True), 1e-05)
            xq = jnp.clip(jnp.round(x * scale), -128.0, 127.0) / scale
            return x + jax.lax.stop_gradient(xq - x)

        def _bitlinear(x, w):
            return jnp.einsum('bsi,oi->bso', _act_quant(x), _weight_quant(w))
        key = jax.random.key(seed)
        k0, k1, k2, k3 = jax.random.split(key, 4)
        x = jax.random.normal(k0, (4, 256, HIDDEN), dtype=jnp.float32)
        w_gate = jax.random.normal(k1, (INNER, HIDDEN), dtype=jnp.float32) / np.sqrt(HIDDEN)
        w_up = jax.random.normal(k2, (INNER, HIDDEN), dtype=jnp.float32) / np.sqrt(HIDDEN)
        w_down = jax.random.normal(k3, (HIDDEN, INNER), dtype=jnp.float32) / np.sqrt(INNER)
        return {'x': x, 'w_gate': w_gate, 'w_up': w_up, 'w_down': w_down}
    _L1_ffn_all = _L1_ffn_setup()
    _L1_ffn_in = {k: v for k, v in _L1_ffn_all.items() if k in ('w_gate', 'w_up', 'w_down')}
    del _L1_ffn_all
    return {'x': x, 'ctx_1024': ctx_1024, 'mask_BxS2_bf1': mask_BxS2_bf1, 'g_xattn': g_xattn, 'g_ffn': g_ffn, 'L0_xattn_wq': _L0_xattn_in['wq'], 'L0_xattn_bq': _L0_xattn_in['bq'], 'L0_xattn_wk': _L0_xattn_in['wk'], 'L0_xattn_bk': _L0_xattn_in['bk'], 'L0_xattn_wv': _L0_xattn_in['wv'], 'L0_xattn_bv': _L0_xattn_in['bv'], 'L0_xattn_wo': _L0_xattn_in['wo'], 'L0_xattn_bo': _L0_xattn_in['bo'], 'L0_ffn_gate_w': _L0_ffn_in['gate_w'], 'L0_ffn_wg': _L0_ffn_in['wg'], 'L0_ffn_wu': _L0_ffn_in['wu'], 'L0_ffn_wd': _L0_ffn_in['wd'], 'L1_xattn_ln_x_g': _L1_xattn_in['ln_x_g'], 'L1_xattn_ln_x_b': _L1_xattn_in['ln_x_b'], 'L1_xattn_ln_l_g': _L1_xattn_in['ln_l_g'], 'L1_xattn_ln_l_b': _L1_xattn_in['ln_l_b'], 'L1_xattn_qn_g': _L1_xattn_in['qn_g'], 'L1_xattn_kn_g': _L1_xattn_in['kn_g'], 'L1_xattn_Wq': _L1_xattn_in['Wq'], 'L1_xattn_Wkv': _L1_xattn_in['Wkv'], 'L1_xattn_Wout': _L1_xattn_in['Wout'], 'L1_xattn_bout': _L1_xattn_in['bout'], 'L1_ffn_w_gate': _L1_ffn_in['w_gate'], 'L1_ffn_w_up': _L1_ffn_in['w_up'], 'L1_ffn_w_down': _L1_ffn_in['w_down']}

def reference(x, ctx_1024, mask_BxS2_bf1, g_xattn, g_ffn, L0_xattn_wq, L0_xattn_bq, L0_xattn_wk, L0_xattn_bk, L0_xattn_wv, L0_xattn_bv, L0_xattn_wo, L0_xattn_bo, L0_ffn_gate_w, L0_ffn_wg, L0_ffn_wu, L0_ffn_wd, L1_xattn_ln_x_g, L1_xattn_ln_x_b, L1_xattn_ln_l_g, L1_xattn_ln_l_b, L1_xattn_qn_g, L1_xattn_kn_g, L1_xattn_Wq, L1_xattn_Wkv, L1_xattn_Wout, L1_xattn_bout, L1_ffn_w_gate, L1_ffn_w_up, L1_ffn_w_down):
    import jax
    import jax.numpy as jnp

    def _L0_xattn_ref(q, k, v, wq, bq, wk, bk, wv, bv, wo, bo):
        import jax, jax.numpy as jnp
        import numpy as np
        import math
        D_MODEL = 128
        N_HEADS = 16
        B, T, D = q.shape
        H = N_HEADS
        n_d = D // H

        def proj(x, w, b):
            y = jnp.einsum('btd,ed->bte', x, w) + b
            return y.reshape(B, T, H, n_d).transpose(0, 2, 1, 3)
        qh, kh, vh = (proj(q, wq, bq), proj(k, wk, bk), proj(v, wv, bv))
        score = jnp.einsum('bhtd,bhsd->bhts', qh, kh) / jnp.sqrt(jnp.float32(n_d))
        causal = jnp.tril(jnp.ones((T, T), bool))
        score = jnp.where(causal, score, -jnp.inf)
        attn = jax.nn.softmax(score, axis=-1)
        out = jnp.einsum('bhts,bhsd->bhtd', attn, vh)
        out = out.transpose(0, 2, 1, 3).reshape(B, T, D)
        return jnp.einsum('btd,ed->bte', out, wo) + bo

    def _L0_ffn_ref(x, gate_w, wg, wu, wd):
        import jax, jax.numpy as jnp
        import numpy as np
        B, S, H = (2, 256, 128)
        E, I, K = (8, 512, 2)

        def _moe_forward(x, gate_w, wg, wu, wd):
            b, s, h = x.shape
            x_flat = x.reshape(-1, h)
            logits = x_flat @ gate_w.T
            top_v, top_i = jax.lax.top_k(logits, K)
            probs = jax.nn.softmax(top_v.astype(jnp.float32), axis=-1).astype(logits.dtype)
            one_hot = jax.nn.one_hot(top_i, E, dtype=probs.dtype)
            combine = jnp.einsum('tk,tke->et', probs, one_hot)

            def body(acc, ws):
                wge, wue, wde, we = ws
                hidden = jax.nn.silu(x_flat @ wge.T) * (x_flat @ wue.T)
                return (acc + we[:, None] * (hidden @ wde.T), None)
            out, _ = jax.lax.scan(body, jnp.zeros_like(x_flat), (wg, wu, wd, combine))
            return out.reshape(b, s, h)
        return _moe_forward(x, gate_w, wg, wu, wd)

    def _L1_xattn_ref(x, latents, mask, ln_x_g, ln_x_b, ln_l_g, ln_l_b, qn_g, kn_g, Wq, Wkv, Wout, bout):
        import jax, jax.numpy as jnp
        import numpy as np
        DIM = 128
        DIM_LATENT = 128
        DIM_HEAD = 64
        HEADS = 16
        INNER = HEADS * DIM_HEAD

        def layernorm(x, g, b, eps=1e-05):
            m = jnp.mean(x, axis=-1, keepdims=True)
            v = jnp.mean((x - m) ** 2, axis=-1, keepdims=True)
            return (x - m) / jnp.sqrt(v + eps) * g + b

        def rmsnorm(x, gamma, eps=1e-08):
            n = jnp.linalg.norm(x, axis=-1, keepdims=True) * x.shape[-1] ** (-0.5)
            return x / jnp.maximum(n, eps) * gamma
        b, n, _ = x.shape
        m = latents.shape[1]
        h, d = (HEADS, DIM_HEAD)
        scale = d ** (-0.5)
        xn = layernorm(x, ln_x_g, ln_x_b)
        ln = layernorm(latents, ln_l_g, ln_l_b)
        q = (ln @ Wq).reshape(b, m, h, d).transpose(0, 2, 1, 3)
        kv = jnp.concatenate([xn @ Wkv, ln @ Wkv], axis=1)
        kv = kv.reshape(b, n + m, 2, h, d)
        k = kv[:, :, 0].transpose(0, 2, 1, 3)
        v = kv[:, :, 1].transpose(0, 2, 1, 3)
        qn = rmsnorm(q, qn_g) * scale
        kn = rmsnorm(k, kn_g)
        sim = jnp.einsum('bhid,bhjd->bhij', qn, kn)
        max_neg = -jnp.finfo(sim.dtype).max
        padded_mask = jnp.concatenate([mask, jnp.ones((b, m), bool)], axis=1)
        sim = jnp.where(padded_mask[:, None, None, :], sim, max_neg)
        attn = jax.nn.softmax(sim.astype(jnp.float32), axis=-1).astype(sim.dtype)
        out = jnp.einsum('bhij,bhjd->bhid', attn, v)
        out = out.transpose(0, 2, 1, 3).reshape(b, m, h * d)
        return out @ Wout + bout

    def _L1_ffn_ref(x, w_gate, w_up, w_down):
        import jax, jax.numpy as jnp
        import numpy as np
        HIDDEN = 128
        INNER = 512

        def _weight_quant(w):
            scale = 1.0 / jnp.clip(jnp.mean(jnp.abs(w)), 1e-05)
            wq = jnp.clip(jnp.round(w * scale), -1.0, 1.0) / scale
            return w + jax.lax.stop_gradient(wq - w)

        def _act_quant(x):
            scale = 127.0 / jnp.clip(jnp.max(jnp.abs(x), axis=-1, keepdims=True), 1e-05)
            xq = jnp.clip(jnp.round(x * scale), -128.0, 127.0) / scale
            return x + jax.lax.stop_gradient(xq - x)

        def _bitlinear(x, w):
            return jnp.einsum('bsi,oi->bso', _act_quant(x), _weight_quant(w))
        gate = jax.nn.silu(_bitlinear(x, w_gate))
        up = _bitlinear(x, w_up)
        return _bitlinear(gate * up, w_down)
    x = x + jnp.tanh(g_xattn[0]) * _L0_xattn_ref(_layernorm(x, axis=-1), ctx_1024, ctx_1024, L0_xattn_wq, L0_xattn_bq, L0_xattn_wk, L0_xattn_bk, L0_xattn_wv, L0_xattn_bv, L0_xattn_wo, L0_xattn_bo)
    x = x + jnp.tanh(g_ffn[0]) * _L0_ffn_ref(_layernorm(x, axis=-1), L0_ffn_gate_w, L0_ffn_wg, L0_ffn_wu, L0_ffn_wd)
    x = x + jnp.tanh(g_xattn[1]) * _L1_xattn_ref(ctx_1024, _layernorm(x, axis=-1), mask_BxS2_bf1, L1_xattn_ln_x_g, L1_xattn_ln_x_b, L1_xattn_ln_l_g, L1_xattn_ln_l_b, L1_xattn_qn_g, L1_xattn_kn_g, L1_xattn_Wq, L1_xattn_Wkv, L1_xattn_Wout, L1_xattn_bout)
    x = x + jnp.tanh(g_ffn[1]) * _L1_ffn_ref(_layernorm(x, axis=-1), L1_ffn_w_gate, L1_ffn_w_up, L1_ffn_w_down)
    return x

_drawn_inputs = setup_inputs


def setup_inputs(seed=0):
    import zlib

    import numpy as np

    out = dict(_drawn_inputs(seed))
    spreads = {'g_ffn': (-1.0, 0.6),
     'L0_xattn_bq': (0.0, 0.1),
     'L0_xattn_bk': (0.0, 0.8),
     'L0_xattn_bv': (0.0, 0.1),
     'L0_xattn_bo': (0.0, 0.1),
     'L1_xattn_ln_x_g': (1.0, 0.6),
     'L1_xattn_ln_x_b': (0.0, 0.8),
     'L1_xattn_ln_l_g': (1.0, 0.6),
     'L1_xattn_ln_l_b': (0.0, 0.8),
     'L1_xattn_qn_g': (1.0, 0.6),
     'L1_xattn_kn_g': (1.0, 0.6),
     'L1_xattn_bout': (0.0, 0.1)}
    factors = {}
    for name, (base, spread) in spreads.items():
        noise = np.random.default_rng([zlib.crc32(name.encode()), seed]).standard_normal(out[name].shape)
        drawn = base * np.exp(spread * noise) if base else spread * noise
        out[name] = jnp.asarray(drawn.astype(out[name].dtype))
    for name, factor in factors.items():
        out[name] = (out[name] * factor).astype(out[name].dtype)
    return out
```

```python
from contextlib import ExitStack

import concourse.bass as bass
from concourse import mybir

P = 128
B, S, D = 128, 64, 128
NT = B * S // P
UN = 4
EPS = 1e-5
H0, D0 = 16, 8
E, I = 8, 512
H1, D1 = 16, 64
INNER = H1 * D1
HID = 512
FAR = -1e30
ROUND = 12582912.0

F32 = mybir.dt.float32
BF16 = mybir.dt.bfloat16
U8 = mybir.dt.uint8
U32 = mybir.dt.uint32
ALU = mybir.AluOpType
ACT = mybir.ActivationFunctionType
AX = mybir.AxisListType


def live(s, lag, count=NT):
    return not isinstance(s, int) or 0 <= s - lag < count


def since(s, lag):
    return not isinstance(s, int) or s >= lag


def slots(eng, body, lags, count=NT, un=UN):
    first = -(-(lags + 2) // un)
    for s in range(first * un):
        body(s, s % un)
    with eng.Fori(first, count // un) as j:
        for k in range(un):
            body(j * un + k, k)
    for s in range(count, count + lags):
        body(s, s % un)


def turn(t, k, un=UN):
    return (t - k) * (16 // un) + 16


class Mem:

    def __init__(self, nc, ctx, stage=""):
        self.nc, self.ctx, self.stage = nc, ctx, stage

    def sb(self, name, shape, dt=F32):
        return self.ctx.enter_context(self.nc.sbuf_tensor(self.stage + name, shape, dt))

    def ps(self, name):
        return self.ctx.enter_context(self.nc.psum_tensor(self.stage + name, [P, 512], F32))

    def sem(self, name):
        return self.ctx.enter_context(self.nc.semaphore(name))


def rows(ap, k=P):
    return ap.rearrange("(a n) -> a n", a=1).partition_broadcast(k)


def setup(nc, m, a):
    ident = m.sb("ident", [P, P])
    ident_b = m.sb("ident_b", [P, P], BF16)
    causal = m.sb("causal", [P, S], BF16)
    head_mask = m.sb("head_mask", [P, H0])
    half_pow = m.sb("half_pow", [P, 16])
    ones_row = m.sb("ones_row", [1, P])
    gates = m.sb("gates", [P, 4])
    tanhs = m.sb("tanhs", [P, 4])
    with ExitStack() as ctx:
        t = Mem(nc, ctx)
        filled, picked, gates_in = t.sem("filled"), t.sem("picked"), t.sem("gates_in")
        block = ctx.enter_context(nc.Block())

        @block.sync
        def _(sp):
            sp.dma_start(gates[:, 0:2], rows(a["g_xattn"])).then_inc(gates_in, 16)
            sp.dma_start(gates[:, 2:4], rows(a["g_ffn"])).then_inc(gates_in, 16)

        @block.gpsimd
        def _(pool):
            pool.memset(ident[:], 0.0).then_inc(filled, 1)
            pool.memset(ident_b[:], 0.0).then_inc(filled, 1)
            pool.memset(causal[:], 0.0).then_inc(filled, 1)
            pool.memset(head_mask[:], 1.0).then_inc(filled, 1)
            pool.memset(half_pow[:], -0.5).then_inc(filled, 1)
            pool.memset(ones_row[:], 1.0).then_inc(filled, 1)
            pool.wait_ge(filled, 6)
            pool.affine_select(out=ident[:], in_=ident[:], compare_op=ALU.not_equal, fill=1.0,
                               base=0, pattern=[[-1, P]], channel_multiplier=1).then_inc(picked, 1)
            pool.affine_select(out=ident_b[:], in_=ident_b[:], compare_op=ALU.not_equal, fill=1.0,
                               base=0, pattern=[[-1, P]], channel_multiplier=1).then_inc(picked, 1)
            for h in range(2):
                c = causal[h * S:(h + 1) * S, :]
                pool.wait_ge(picked, 2 + h)
                pool.affine_select(out=c, in_=c, compare_op=ALU.is_ge, fill=FAR, base=0,
                                   pattern=[[-1, S]], channel_multiplier=1).then_inc(picked, 1)
            pool.wait_ge(picked, 4)
            pool.affine_select(out=head_mask[:], in_=head_mask[:], compare_op=ALU.is_ge, fill=0.0,
                               base=0, pattern=[[-D0, H0]], channel_multiplier=1).then_inc(picked, 1)
            pool.wait_ge(picked, 5)
            pool.affine_select(out=head_mask[:], in_=head_mask[:], compare_op=ALU.is_ge, fill=0.0,
                               base=D0 - 1, pattern=[[D0, H0]], channel_multiplier=-1).then_inc(picked, 1)

        @block.scalar
        def _(act):
            act.wait_ge(gates_in, 32)
            act.activation(tanhs[:], gates[:], ACT.Tanh)

    return dict(ident=ident, ident_b=ident_b, causal=causal, head_mask=head_mask,
                half_pow=half_pow, ones_row=ones_row, tanhs=tanhs)


def causal_attention(nc, c, xres, a):
    LAGS = 6
    with ExitStack() as ctx:
        m = Mem(nc, ctx, "attn_")
        wqT, wkT, wvT, woT = (m.sb(n, [P, D]) for n in ("wqT", "wkT", "wvT", "woT"))
        bq, bk = m.sb("bq", [P, 1]), m.sb("bk", [P, 1])
        bv, bo = m.sb("bv", [1, D]), m.sb("bo", [1, D])
        context = m.sb("context", [P, UN, D])
        stats = m.sb("stats", [P, 2, 6])
        mean_var = m.sb("mean_var", [P, 2, 2])
        var_eps = m.sb("var_eps", [P, 2, 1])
        rstd = m.sb("rstd", [P, 2, 1])
        z = m.sb("z", [P, 2, D])
        xT = m.sb("xT", [P, 2, P])
        cT = m.sb("cT", [P, 2, 2, 2, S])
        qT = m.sb("qT", [P, UN, P])
        kT = m.sb("kT", [P, 2, P])
        k_wide = m.sb("k_wide", [P, 2, H0, P])
        v_wide = m.sb("v_wide", [P, UN, 2, H0 // 2, 2 * D0 + 2])
        peak = m.sb("peak", [P, 2, H0])
        below = m.sb("below", [P, 2, H0, S])
        probs = m.sb("probs", [P, 2, H0, S])
        probsT = m.sb("probsT", [P, 2, 8, P])
        rsum = m.sb("rsum", [P, 2, H0])
        o = m.sb("o", [P, 2, D])
        oT = m.sb("oT", [P, 2, P])

        ps_T, ps_qkv, ps_o, ps_out = (m.ps(n) for n in ("ps_T", "ps_qkv", "ps_o", "ps_out"))
        ps_s = [m.ps("ps_s0"), m.ps("ps_s1")]
        ps_pT = [m.ps("ps_pT0"), m.ps("ps_pT1")]
        o_ps = ps_o[:, 0:8 * 18].rearrange("p (c w) -> p c w", w=18)

        w_in = m.sem("a_w_in")
        context_in = [m.sem(f"a_context_in{k}") for k in range(UN)]
        (v_cleared, stats_done, mv_done, eps_added, rstd_done, z_done, xc_turned, xc_copied, qkv_made,
         qk_copied, v_copied, k_widened, scores_done, peaks_done, below_done, probs_done,
         probs_turned, probsT_copied, pv_done, rsum_done, o_done, o_turned, oT_copied, out_made,
         x_done) = (m.sem("a_" + n) for n in (
            "v_cleared", "stats_done", "mv_done", "eps_added", "rstd_done", "z_done", "xc_turned",
            "xc_copied", "qkv_made", "qk_copied", "v_copied", "k_widened",
            "scores_done", "peaks_done", "below_done", "probs_done", "probs_turned",
            "probsT_copied", "pv_done", "rsum_done", "o_done", "o_turned", "oT_copied",
            "out_made", "x_done"))
        block = ctx.enter_context(nc.Block())

        @block.sync
        def _(sp):
            for dst, src in ((wqT, "L0_xattn_wqT"), (wkT, "L0_xattn_wkT"), (wvT, "L0_xattn_wvT"),
                             (woT, "L0_xattn_woT")):
                sp.dma_start(dst[:], a[src]).then_inc(w_in, 16)
            for dst, src in ((bq, "L0_xattn_bq"), (bk, "L0_xattn_bk")):
                sp.dma_start(dst[:], a[src].rearrange("(p o) -> p o", o=1)).then_inc(w_in, 16)
            for dst, src in ((bv, "L0_xattn_bv"), (bo, "L0_xattn_bo")):
                sp.dma_start(dst[:], a[src].rearrange("(o n) -> o n", o=1)).then_inc(w_in, 16)

            def body(s, k):
                if live(s, 0):
                    if since(s, UN):
                        sp.wait_ge(xc_turned, s - UN + 1)
                    sp.dma_start(context[:, k, :], a["ctx"][bass.ds(s, 1)].rearrange("o p d -> p (o d)")
                                 ).then_inc(context_in[k], 16)

            slots(sp, body, 0)

        @block.vector
        def _(dve):
            dve.memset(v_wide[:], 0.0).then_inc(v_cleared, 1)
            dve.wait_ge(v_cleared, 1)
            for h in range(2):
                dve.memset(v_wide[h * S:(h + 1) * S, :, :, :, 2 * D0 + h:2 * D0 + h + 1],
                           1.0).then_inc(v_cleared, 1)

            def body(s, k):
                if live(s, 5):
                    t, b = s - 5, (k - 5) % 2
                    dve.wait_ge(pv_done, t + 1)
                    dve.reciprocal(rsum[:, b, :].rearrange("p (c h) -> p c h", h=2),
                                   o_ps[:, :, 16:18]).then_inc(rsum_done, 1)
                    dve.wait_ge(rsum_done, t + 1)
                    if since(t, 2):
                        dve.wait_ge(o_turned, t - 1)
                    dve.tensor_tensor(
                        o[:, b, :].rearrange("p (c h d) -> p c h d", d=D0, h=2),
                        o_ps[:, :, 0:16].rearrange("p c (h d) -> p c h d", d=D0),
                        rsum[:, b, :].rearrange("p (c h o) -> p c h o", h=2, o=1).broadcast_to([P, 8, 2, D0]),
                        ALU.mult).then_inc(o_done, 1)
                if live(s, 6):
                    t = s - 6
                    dve.wait_ge(out_made, t + 1)
                    xt = xres[:, bass.ds(t, 1), :]
                    dve.scalar_tensor_tensor(xt, ps_out[:, P:2 * P].rearrange("p (o d) -> p o d", o=1),
                                             c["tanhs"][:, 0:1], xt,
                                             ALU.mult, ALU.add).then_inc(x_done, 1)
                if live(s, 0):
                    b = k % 2
                    b0 = k % 2
                    dve.bn_stats(stats[:, b0, :], xres[:, bass.ds(s, 1), :]).then_inc(stats_done, 1)
                if live(s, 3):
                    t, b = s - 3, (k - 3) % 2
                    if live(s, 0):
                        dve.wait_ge(stats_done, s + 1)
                    for g in range(2):
                        dve.wait_ge(scores_done, 2 * t + g + 1)
                        sc = ps_s[g][:].rearrange("p (h n) -> p h n", n=S)
                        dve.tensor_reduce(peak[:, b, 8 * g:8 * g + 8], sc, AX.X, ALU.max).then_inc(peaks_done, 1)
                        dve.wait_ge(peaks_done, 2 * t + g + 1)
                        if since(t, 2) and g == 0:
                            dve.wait_ge(probs_done, t - 1)
                        dve.tensor_tensor(below[:, b, 8 * g:8 * g + 8, :], sc,
                                          peak[:, b, 8 * g:8 * g + 8].rearrange("p (h o) -> p h o", o=1)
                                          .broadcast_to([P, 8, S]), ALU.subtract).then_inc(below_done, 1)
                if live(s, 0):
                    if isinstance(s, int):
                        dve.wait_ge(stats_done, s + 1)
                    dve.bn_aggr(mean_var[:, b0, :], stats[:, b0, :]).then_inc(mv_done, 1)
                    dve.wait_ge(mv_done, s + 1)
                    dve.tensor_scalar(var_eps[:, b0, :], mean_var[:, b0, 1:2], EPS, None,
                                      ALU.add).then_inc(eps_added, 1)
                if live(s, 0):
                    b = k % 2
                    dve.wait_ge(rstd_done, s + 1)
                    if since(s, 2):
                        dve.wait_ge(xc_turned, s - 1)
                    dve.tensor_scalar(z[:, b, :], xres[:, bass.ds(s, 1), :].rearrange("p o d -> p (o d)"),
                                      mean_var[:, b, 0:1], rstd[:, b, :],
                                      ALU.subtract, ALU.mult).then_inc(z_done, 1)

            slots(dve, body, LAGS)

        @block.gpsimd
        def _(pool):
            def body(s, k):
                if live(s, 0):
                    b = k % 2
                    pool.wait_ge(eps_added, s + 1)
                    pool.tensor_tensor(rstd[:, b, :], var_eps[:, b, :], c["half_pow"][:, 0:1],
                                       ALU.pow).then_inc(rstd_done, 1)
                if live(s, 2):
                    t, b = s - 2, (k - 2) % 2
                    pool.wait_ge(qk_copied, 2 * (t + 1))
                    if since(t, 2):
                        pool.wait_ge(scores_done, 2 * (t - 1))
                    pool.tensor_tensor(
                        k_wide[:, b], kT[:, b:b + 1, :].broadcast_to([P, H0, P]),
                        c["head_mask"][:].rearrange("p (h o) -> p h o", o=1).broadcast_to([P, H0, P]),
                        ALU.mult).then_inc(k_widened, 1)

            slots(pool, body, LAGS)

        @block.scalar
        def _(act):
            act.wait_ge(v_cleared, 3)
            act.wait_ge(w_in, 8 * 16)

            def body(s, k):
                if live(s, 1):
                    t, b = s - 1, (k - 1) % 2
                    act.wait_ge(xc_turned, t + 1)
                    if since(t, 2):
                        act.wait_ge(qkv_made, t - 1)
                    act.copy(xT[:, b, :], ps_T[:, 0:P]).then_inc(xc_copied, 1)
                    act.copy(cT[:, b], ps_T[:, P:2 * P].rearrange("p (q o n) -> p q o n", q=2, o=1)
                             .broadcast_to([P, 2, 2, S])).then_inc(xc_copied, 1)
                    act.wait_ge(qkv_made, t + 1)
                    if since(t, 2):
                        act.wait_ge(k_widened, t - 1)
                    act.activation(kT[:, b, :], ps_qkv[:, P:2 * P], ACT.Identity,
                                   bias=bk[:]).then_inc(qk_copied, 1)
                    if since(t, 4):
                        act.wait_ge(pv_done, t - 3)
                    kt = (k - 1) % UN
                    act.activation(qT[:, kt, :], ps_qkv[:, 0:P], ACT.Identity,
                                   bias=bq[:]).then_inc(qk_copied, 1)
                    for h in range(2):
                        r = slice(h * S, (h + 1) * S)
                        act.copy(v_wide[r, kt, :, :, h * D0:(h + 1) * D0],
                                 ps_qkv[r, 2 * P:4 * P].rearrange("p (b c h d) -> p b c h d", b=2, c=8, h=2)
                                 [:, :, :, h, :]).then_inc(v_copied, 1)
                if live(s, 4):
                    t, b = s - 4, (k - 4) % 2
                    for g in range(2):
                        act.wait_ge(probs_turned, 2 * t + g + 1)
                        if since(t, 2) and g == 0:
                            act.wait_ge(pv_done, t - 1)
                        act.copy(probsT[:, b, 4 * g:4 * g + 4, :].rearrange("p c n -> p (c n)"),
                                 ps_pT[g][:]).then_inc(probsT_copied, 1)
                if live(s, 5):
                    t, b = s - 5, (k - 5) % 2
                    act.wait_ge(o_turned, t + 1)
                    if since(t, 2):
                        act.wait_ge(out_made, t - 1)
                    act.copy(oT[:, b, :], ps_out[:, 0:P]).then_inc(oT_copied, 1)
                if live(s, 3):
                    t, b = s - 3, (k - 3) % 2
                    act.wait_ge(below_done, 2 * (t + 1))
                    if since(t, 2):
                        act.wait_ge(probs_turned, 2 * (t - 1))
                    act.activation(probs[:, b], below[:, b], ACT.Exp, scale=D0 ** -0.5).then_inc(probs_done, 1)

            slots(act, body, LAGS)

        @block.tensor
        def _(pe):
            pe.wait_ge(w_in, 8 * 16)

            def body(s, k):
                if live(s, 1):
                    t, b, kt = s - 1, (k - 1) % 2, (k - 1) % UN
                    pe.wait_ge(z_done, t + 1)
                    if since(t, 1):
                        pe.wait_ge(xc_copied, 2 * t)
                    pe.transpose(ps_T[:, 0:P], z[:, b, :], c["ident"][:])
                    pe.wait_ge(context_in[kt], turn(t, kt))
                    pe.transpose(ps_T[:, P:2 * P], context[:, kt, :], c["ident"][:]).then_inc(xc_turned, 1)
                if live(s, 3):
                    t, b, kt = s - 3, (k - 3) % 2, (k - 3) % UN
                    pe.wait_ge(k_widened, t + 1)
                    pe.wait_ge(qk_copied, 2 * (t + 1))
                    for g in range(2):
                        if since(t, 1):
                            pe.wait_ge(below_done, 2 * t - 1 + g)
                        pe.matmul(ps_s[g][:], c["ident_b"][:],
                                  c["causal"][:].rearrange("p (o n) -> p o n", o=1).broadcast_to([P, 8, S]),
                                  start=True, stop=True, skip_group_check=True)
                        for q in range(2):
                            mm = pe.matmul(ps_s[g][q * S:(q + 1) * S, :], qT[:, kt, q * S:(q + 1) * S],
                                           k_wide[:, b, 8 * g:8 * g + 8, q * S:(q + 1) * S],
                                           start=False, stop=True, skip_group_check=True)
                        mm.then_inc(scores_done, 1)
                if live(s, 1):
                    t, b = s - 1, (k - 1) % 2
                    pe.wait_ge(xc_copied, 2 * (t + 1))
                    if since(t, 1):
                        pe.wait_ge(qk_copied, 2 * t)
                        pe.wait_ge(v_copied, 2 * t)
                    pe.matmul(ps_qkv[:, P:2 * P], wkT[:], cT[:, b, :, 0, :], start=True, stop=True)
                    pe.matmul(ps_qkv[:, 0:P], wqT[:], xT[:, b, :], start=True, stop=True)
                    for q in range(2):
                        out = ps_qkv[:, (2 + q) * P:(3 + q) * P]
                        pe.matmul(out, cT[:, b, q].rearrange("p o n -> p (o n)"), wvT[:], start=True, stop=False)
                        mm = pe.matmul(out, c["ones_row"][:], bv[:], start=False, stop=True)
                    mm.then_inc(qkv_made, 1)
                if live(s, 4):
                    t, b = s - 4, (k - 4) % 2
                    pe.wait_ge(probs_done, t + 1)
                    for g in range(2):
                        if since(t, 1):
                            pe.wait_ge(probsT_copied, 2 * t - 1 + g)
                        for j in range(4):
                            h = 8 * g + 2 * j
                            mm = pe.transpose(ps_pT[g][:, j * P:(j + 1) * P],
                                              probs[:, b, h:h + 2, :].rearrange("p h n -> p (h n)"),
                                              c["ident"][:])
                        mm.then_inc(probs_turned, 1)
                if live(s, 5):
                    t, b = s - 5, (k - 5) % 2
                    pe.wait_ge(o_done, t + 1)
                    if since(t, 1):
                        pe.wait_ge(x_done, t)
                    pe.transpose(ps_out[:, 0:P], o[:, b, :], c["ident"][:]).then_inc(o_turned, 1)
                if live(s, 4):
                    t, b, kt = s - 4, (k - 4) % 2, (k - 4) % UN
                    pe.wait_ge(probsT_copied, 2 * (t + 1))
                    pe.wait_ge(v_copied, 2 * (t + 1))
                    if since(t, 1):
                        pe.wait_ge(o_done, t)
                    for q in range(2):
                        for j in range(8):
                            mm = pe.matmul(ps_o[q * S:(q + 1) * S, 18 * j:18 * j + 18],
                                           probsT[:, b, j, q * S:(q + 1) * S],
                                           v_wide[:, kt, q, j, :], start=True, stop=True)
                    mm.then_inc(pv_done, 1)
                if live(s, 5):
                    t, b = s - 5, (k - 5) % 2
                    pe.wait_ge(oT_copied, t + 1)
                    pe.matmul(ps_out[:, P:2 * P], oT[:, b, :], woT[:], start=True, stop=False)
                    pe.matmul(ps_out[:, P:2 * P], c["ones_row"][:], bo[:], start=False, stop=True).then_inc(out_made, 1)

            slots(pe, body, LAGS)


def load_x(nc, xres, a):
    with ExitStack() as ctx:
        m = Mem(nc, ctx)
        x_in = m.sem("x_in")
        block = ctx.enter_context(nc.Block())
        PARTS = 8

        @block.sync
        def _(sp):
            for j in range(PARTS):
                n = NT // PARTS
                sp.dma_start(xres[:, j * n:(j + 1) * n, :],
                             a["x"][j * n:(j + 1) * n].rearrange("t p d -> p t d")).then_inc(x_in, 16)
            sp.wait_ge(x_in, 16 * PARTS)


def store_x(nc, xres, out):
    with ExitStack() as ctx:
        m = Mem(nc, ctx)
        x_out = m.sem("x_out")
        block = ctx.enter_context(nc.Block())
        PARTS = 8

        @block.sync
        def _(sp):
            for j in range(PARTS):
                n = NT // PARTS
                sp.dma_start(out[j * n:(j + 1) * n].rearrange("t p d -> p t d"),
                             xres[:, j * n:(j + 1) * n, :]).then_inc(x_out, 16)
            sp.wait_ge(x_out, 16 * PARTS)


def at(j, k, lag, un):
    return j + (k - lag) // un, (k - lag) % un


def turns(eng, body, lags, count, un):
    first = -(-(lags + 2) // un)
    for j in range(first):
        for k in range(un):
            body(j, k)
    with eng.Fori(first, count // un) as j:
        for k in range(un):
            body(j, k)
    for s in range(count, count + lags):
        body(s // un, s % un)


def split_weights(nc, name, m, loads):
    with ExitStack() as ctx:
        t = Mem(nc, ctx)
        size = max(src.shape[-1] for _, _, parts in loads for _, src in parts)
        raw = t.sb(name + "_raw", [P, 2, size])
        raw_in = [t.sem(f"{name}_raw_in{k}") for k in range(2)]
        high_done, low_done = t.sem(name + "_high_done"), t.sem(name + "_low_done")
        jobs = [(hi, lo, cols, src) for hi, lo, parts in loads for cols, src in parts]
        block = ctx.enter_context(nc.Block())

        @block.sync
        def _(sp):
            for n, (_, _, cols, src) in enumerate(jobs):
                if n >= 2:
                    sp.wait_ge(low_done, n - 1)
                sp.dma_start(raw[:, n % 2, 0:src.shape[-1]], src).then_inc(raw_in[n % 2], 16)

        @block.scalar
        def _(act):
            for n, (hi, _, cols, src) in enumerate(jobs):
                act.wait_ge(raw_in[n % 2], 16 * (n // 2 + 1))
                act.copy(hi[:, cols], raw[:, n % 2, 0:src.shape[-1]]).then_inc(high_done, 1)

        @block.vector
        def _(dve):
            for n, (hi, lo, cols, src) in enumerate(jobs):
                dve.wait_ge(high_done, n + 1)
                dve.tensor_tensor(lo[:, cols], raw[:, n % 2, 0:src.shape[-1]], hi[:, cols],
                                  ALU.subtract).then_inc(low_done, 1)


def perceiver(nc, c, xres, a):
    UNG, G, HALF = 8, 4 * NT, 512
    LAGS = 13
    with ExitStack() as ctx:
        m = Mem(nc, ctx, "perc_")
        wq_h, wq_l = m.sb("wq_h", [P, INNER], BF16), m.sb("wq_l", [P, INNER], BF16)
        wkv_h, wkv_l = m.sb("wkv_h", [P, 2 * INNER], BF16), m.sb("wkv_l", [P, 2 * INNER], BF16)
        w_out = m.sb("w_out", [P, H1 // 2, D])
        split_weights(nc, "c", m, [(wq_h, wq_l, [(slice(0, INNER), a["L1_xattn_Wq"])]),
                                   (wkv_h, wkv_l, [(slice(0, INNER), a["L1_xattn_Wkv"][:, 0:INNER]),
                                                   (slice(INNER, 2 * INNER),
                                                    a["L1_xattn_Wkv"][:, INNER:2 * INNER])])])
        gain = m.sb("gain", [P, 2])
        shift = m.sb("shift", [P, 2])
        norm_gains = m.sb("norm_gains", [P, 2])
        qk_gain = m.sb("qk_gain", [P, 1])
        b_out = m.sb("b_out", [1, D])
        ones_b = m.sb("ones_b", [1, P], BF16)
        context = m.sb("context2", [P, 2, D])
        mask_in = m.sb("mask_in", [1, 2, 2, S], U8)
        mask_row = m.sb("mask_row", [1, 2, 2, P], BF16)
        stats = m.sb("stats2", [P, 2, 2, 6])
        mean_var = m.sb("mean_var2", [P, 2, 2, 2])
        var_eps = m.sb("var_eps2", [P, 2, 2])
        rstd = m.sb("rstd2", [P, 2, 2])
        z = m.sb("z2", [P, 2, 2, D])
        zT = m.sb("zT", [P, 2, 2, P])
        keys_h, keys_l = (m.sb(n, [P, 2, 2, P], BF16) for n in ("keys_h", "keys_l"))
        lat_h, lat_l = (m.sb(n, [P, 2, P], BF16) for n in ("lat_h", "lat_l"))
        squares = m.sb("squares", [P, 3, HALF])
        square_sums = m.sb("square_sums", [P, 3, 8])
        rnorm = m.sb("rnorm", [P, 3, 8])
        qk_n = m.sb("qk_n", [P, 3, HALF])
        kT = m.sb("kT2", [P, 2, 4, P])
        q_diag = m.sb("q_diag", [P, 2, 4, 2, P])
        v = m.sb("v", [P, 4, HALF])
        neg_peak = m.sb("neg_peak", [P, 2, 4])
        sums = m.sb("sums", [P, 2, 4])
        rsum = m.sb("rsum2", [P, 2, 4])
        probs = m.sb("probs2", [P, 2, 4, P])
        probs_n = m.sb("probs_n", [P, 2, 4, P])
        probsT = m.sb("probsT2", [P, 2, 4, P])
        oT = m.sb("oT2", [P, 2, H1 // 2, 2, S])

        ps_kq = [m.ps(f"ps_kq{i}") for i in range(3)]
        ps_s = [m.ps("ps_s0"), m.ps("ps_s1")]
        ps_vp, ps_o = m.ps("ps_vp"), m.ps("ps_o")
        ps_t = m.ps("ps_t")

        w_in = m.sem("c_w_in")
        tile_in = [m.sem(f"c_tile_in{k}") for k in range(2)]
        names = ("ready", "stats_done", "mv_done", "eps_added", "rstd_done", "z_done", "z_turned", "zT_done",
                 "keys_h_done", "keys_l_done", "lat_done", "mask_done", "kq_made", "squared", "reduced",
                 "rnorm_done", "kq_normed", "v_made", "v_copied", "k_turned", "q_turned",
                 "kT_copied", "q_copied", "scores_done", "peaks_done", "probs_done", "rsum_done",
                 "probs_normed", "probs_turned", "probsT_copied", "o_made", "o_copied", "y_made", "x_done")
        sem = {n: m.sem("c_" + n) for n in names}
        (ready, stats_done, mv_done, eps_added, rstd_done, z_done, z_turned, zT_done,
         keys_h_done, keys_l_done, lat_done, mask_done, kq_made, squared, reduced,
         rnorm_done, kq_normed, v_made, v_copied, k_turned, q_turned,
         kT_copied, q_copied, scores_done, peaks_done, probs_done, rsum_done,
         probs_normed, probs_turned, probsT_copied, o_made, o_copied, y_made, x_done) = (sem[n] for n in names)
        NW = 10
        block = ctx.enter_context(nc.Block())

        def group(j, k, lag):
            j, k = at(j, k, lag, UNG)
            g = j * UNG + k
            return not isinstance(j, int) or 0 <= g < G, j, k, g

        def past(x, least):
            return not isinstance(x, int) or x >= least

        def use(j, k, keys):
            return 12 * j + 3 * (k // 2) + (0 if not keys else 1 + k % 2)

        @block.sync
        def _(sp):
            sp.dma_start(w_out[:], a["L1_xattn_Wout"].rearrange("(c p) n -> p c n", p=P)).then_inc(w_in, 16)
            for col, (g_, b_) in enumerate((("ln_x_g", "ln_x_b"), ("ln_l_g", "ln_l_b"))):
                sp.dma_start(gain[:, col:col + 1], a["L1_xattn_" + g_].rearrange("(p o) -> p o", o=1)).then_inc(w_in, 16)
                sp.dma_start(shift[:, col:col + 1], a["L1_xattn_" + b_].rearrange("(p o) -> p o", o=1)).then_inc(w_in, 16)
            for h in range(2):
                for col, n in enumerate(("qn_g", "kn_g")):
                    sp.dma_start(norm_gains[h * D1:(h + 1) * D1, col:col + 1],
                                 a["L1_xattn_" + n].rearrange("(p o) -> p o", o=1)).then_inc(w_in, 16)
            sp.dma_start(b_out[:], a["L1_xattn_bout"].rearrange("(o n) -> o n", o=1)).then_inc(w_in, 16)

            def body(t, b):
                if past(t, 2):
                    sp.wait_ge(z_done, 2 * (t - 1))
                    sp.wait_ge(mask_done, t - 1)
                sp.dma_start(context[:, b, :], a["ctx"][bass.ds(t, 1)].rearrange("o p d -> p (o d)")
                             ).then_inc(tile_in[b], 16)
                sp.dma_start(mask_in[:, b], a["mask"][bass.ds(t * 2, 2)].rearrange("(o b) n -> o b n", o=1)
                             ).then_inc(tile_in[b], 16)

            for t in range(2):
                body(t, t)
            with sp.Fori(1, NT // 2) as j:
                for b in range(2):
                    body(j * 2 + b, b)

        @block.gpsimd
        def _(pool):
            pool.memset(mask_row[:], 0.0).then_inc(ready, 1)
            pool.memset(ones_b[:], 1.0).then_inc(ready, 1)
            pool.wait_ge(ready, 4)

            def body(j, k):
                ok, jj, kk, g = group(j, k, 3)
                if ok:
                    for keys in ([False, True] if kk % 2 == 0 else [True]):
                        n = use(jj, kk, keys)
                        pool.wait_ge(reduced, n + 1)
                        b = use(0, kk, keys) % 3
                        pool.tensor_tensor(rnorm[:, b], square_sums[:, b], c["half_pow"][:, 0:8],
                                           ALU.pow).then_inc(rnorm_done, 1)
                ok, jj, kk, g = group(j, k, 0)
                if ok and kk % 4 == 0:
                    t, b = 2 * jj + kk // 4, kk // 4
                    pool.wait_ge(eps_added, 2 * (t + 1))
                    pool.tensor_tensor(rstd[:, b, :], var_eps[:, b, :], c["half_pow"][:, 0:2],
                                       ALU.pow).then_inc(rstd_done, 1)
                ok, jj, kk, g = group(j, k, 2)
                if ok and kk % 4 == 0:
                    t, b = 2 * jj + kk // 4, kk // 4
                    pool.wait_ge(keys_h_done, t + 1)
                    pool.tensor_tensor(keys_l[:, b].rearrange("p q (s n) -> p s q n", s=2),
                                       zT[:, b].rearrange("p s (q n) -> p s q n", q=2),
                                       keys_h[:, b].rearrange("p q (s n) -> p s q n", s=2),
                                       ALU.subtract).then_inc(keys_l_done, 1)
                    pool.tensor_copy(lat_h[:, b].rearrange("p (q n) -> p q n", q=2),
                                     keys_h[:, b, :, S:P]).then_inc(lat_done, 1)
                    pool.wait_ge(lat_done, 2 * t + 1)
                    pool.tensor_tensor(lat_l[:, b], zT[:, b, 1], lat_h[:, b], ALU.subtract).then_inc(lat_done, 1)

            turns(pool, body, LAGS, G, UNG)

        @block.scalar
        def _(act):
            act.wait_ge(w_in, 16 * NW)
            act.wait_ge(ready, 4)

            def copy_keys(kk, g):
                act.wait_ge(k_turned, g + 1)
                if past(g, 2):
                    act.wait_ge(scores_done, g - 1)
                act.copy(kT[:, kk % 2].rearrange("p u n -> p (u n)"), ps_t[:]).then_inc(kT_copied, 1)

            def body(j, k):
                ok, jj, kk, g = group(j, k, 5)
                if ok and kk % 2 == 0:
                    pair, hb = 4 * jj + kk // 2, (kk // 2) % 2
                    act.wait_ge(q_turned, pair + 1)
                    if past(pair, 2):
                        act.wait_ge(scores_done, 2 * (pair - 1))
                    for h in range(2):
                        r = slice(h * S, (h + 1) * S)
                        act.activation(q_diag[r, hb, :, :, h * S:(h + 1) * S],
                                       ps_t[r, :].rearrange("p (u q n) -> p u q n", u=4, q=2),
                                       ACT.Identity, scale=qk_gain[r, :]).then_inc(q_copied, 1)
                if ok and kk % 2 == 1:
                    copy_keys(kk, g)
                ok, jj, kk, g = group(j, k, 7)
                if ok:
                    act.wait_ge(v_made, g + 1)
                    if past(g, 4):
                        act.wait_ge(o_made, g - 3)
                    act.copy(v[:, kk % 4], ps_vp[:]).then_inc(v_copied, 1)
                ok, jj, kk, g = group(j, k, 2)
                if ok and kk % 4 == 0:
                    t, b = 2 * jj + kk // 4, kk // 4
                    act.wait_ge(z_turned, t + 1)
                    if past(t, 2):
                        act.wait_ge(lat_done, 2 * (t - 1))
                    for src in range(2):
                        act.activation(zT[:, b, src], ps_t[:, src * P:(src + 1) * P], ACT.Identity,
                                       bias=shift[:, src:src + 1], scale=gain[:, src:src + 1]).then_inc(zT_done, 1)
                    act.wait_ge(zT_done, 2 * (t + 1))
                    if past(t, 2):
                        act.wait_ge(v_made, 4 * (t - 1))
                    act.copy(keys_h[:, b].rearrange("p q (s n) -> p s q n", s=2),
                             zT[:, b].rearrange("p s (q n) -> p s q n", q=2)).then_inc(keys_h_done, 1)
                ok, jj, kk, g = group(j, k, 7)
                if ok:
                    b = kk % 2
                    act.wait_ge(peaks_done, g + 1)
                    if past(g, 2):
                        act.wait_ge(probs_normed, 4 * (g - 1))
                    for u in range(4):
                        act.activation(probs[:, b, u], ps_s[b][:, u * P:(u + 1) * P], ACT.Exp,
                                       bias=neg_peak[:, b, u:u + 1],
                                       accum_out=sums[:, b, u:u + 1]).then_inc(probs_done, 1)
                ok, jj, kk, g = group(j, k, 5)
                if ok and kk % 2 == 0:
                    copy_keys(kk, g)
                ok, jj, kk, g = group(j, k, 3)
                if ok:
                    for keys in ([False, True] if kk % 2 == 0 else [True]):
                        n, b = use(jj, kk, keys), use(0, kk, keys) % 3
                        act.wait_ge(kq_made, n + 1)
                        if past(n, 3):
                            act.wait_ge(reduced, n - 2)
                        act.square(squares[:, b], ps_kq[b][:]).then_inc(squared, 1)
                ok, jj, kk, g = group(j, k, 8)
                if ok:
                    b = kk % 2
                    act.wait_ge(probs_turned, g + 1)
                    if past(g, 2):
                        act.wait_ge(o_made, g - 1)
                    act.copy(probsT[:, b].rearrange("p u n -> p (u n)"), ps_vp[:]).then_inc(probsT_copied, 1)

            turns(act, body, LAGS, G, UNG)

        @block.vector
        def _(dve):
            dve.memset(q_diag[:], 0.0).then_inc(ready, 1)
            dve.wait_ge(w_in, 16 * NW)
            dve.scalar_tensor_tensor(qk_gain[:], norm_gains[:, 0:1], D1 ** -0.5 * D1, norm_gains[:, 1:2],
                                     ALU.mult, ALU.mult).then_inc(ready, 1)

            def body(j, k):
                ok, jj, kk, g = group(j, k, 3)
                if ok and kk % 4 == 0:
                    t, b = 2 * jj + kk // 4, kk // 4
                    dve.wait_ge(tile_in[b], 32 * (jj + 1))
                    if past(t, 2):
                        dve.wait_ge(scores_done, 4 * (t - 1))
                    dve.tensor_scalar(mask_row[:, b, :, 0:S], mask_in[:, b], -FAR, FAR,
                                       ALU.mult, ALU.add).then_inc(mask_done, 1)
                ok, jj, kk, g = group(j, k, 7)
                if ok:
                    b = kk % 2
                    dve.wait_ge(scores_done, g + 1)
                    dve.tensor_reduce(neg_peak[:, b], ps_s[b][:].rearrange("p (u n) -> p u n", u=4), AX.X,
                                      ALU.max, negate=True).then_inc(peaks_done, 1)
                ok, jj, kk, g = group(j, k, 8)
                if ok:
                    b = kk % 2
                    dve.wait_ge(probs_done, 4 * (g + 1))
                    dve.reciprocal(rsum[:, b], sums[:, b]).then_inc(rsum_done, 1)
                    dve.wait_ge(rsum_done, g + 1)
                    if past(g, 2):
                        dve.wait_ge(probs_turned, g - 1)
                    for u in range(4):
                        dve.tensor_scalar(probs_n[:, b, u], probs[:, b, u], rsum[:, b, u:u + 1], None,
                                          ALU.mult).then_inc(probs_normed, 1)
                ok, jj, kk, g = group(j, k, 1)
                if ok and kk % 4 == 0:
                    t, b = 2 * jj + kk // 4, kk // 4
                    xt = xres[:, bass.ds(t, 1), :].rearrange("p o d -> p (o d)")
                    dve.wait_ge(rstd_done, t + 1)
                    if past(t, 2):
                        dve.wait_ge(z_turned, t - 1)
                    for src, rows_ in enumerate((context[:, b, :], xt)):
                        dve.tensor_scalar(z[:, b, src], rows_, mean_var[:, b, src, 0:1], rstd[:, b, src:src + 1],
                                          ALU.subtract, ALU.mult).then_inc(z_done, 1)
                ok, jj, kk, g = group(j, k, 0)
                if ok and kk % 4 == 0:
                    t, b = 2 * jj + kk // 4, kk // 4
                    xt = xres[:, bass.ds(t, 1), :].rearrange("p o d -> p (o d)")
                    dve.wait_ge(tile_in[b], 32 * (jj + 1))
                    dve.bn_stats(stats[:, b, 0], context[:, b, :]).then_inc(stats_done, 1)
                    dve.bn_stats(stats[:, b, 1], xt).then_inc(stats_done, 1)
                stats_of = (2 * jj + kk // 4) if ok and kk % 4 == 0 else None
                ok, jj, kk, g = group(j, k, 9)
                if ok:
                    tb, half, q = kk // 4, (kk // 2) % 2, kk % 2
                    if stats_of is not None:
                        dve.wait_ge(stats_done, 2 * (stats_of + 1))
                    dve.wait_ge(o_made, g + 1)
                    if kk % 4 == 0 and past(g, 8):
                        dve.wait_ge(y_made, 2 * jj + kk // 4 - 1)
                    for h in range(2):
                        r = slice(h * S, (h + 1) * S)
                        dve.tensor_copy(oT[r, tb, 4 * half:4 * half + 4, q, :],
                                        ps_o[r, :].rearrange("p (u h n) -> p u h n", u=4, h=2)[:, :, h, :]
                                        ).then_inc(o_copied, 1)
                ok, jj, kk, g = group(j, k, 4)
                for keys in [] if not ok else [False, True] if kk % 2 == 0 else [True]:
                    n, b = use(jj, kk, keys), use(0, kk, keys) % 3
                    dve.wait_ge(rnorm_done, n + 1)
                    if not keys and past(jj * 4 + kk // 2, 1):
                        dve.wait_ge(q_turned, jj * 4 + kk // 2)
                    if keys and past(g, 2):
                        dve.wait_ge(k_turned, g - 1)
                    dve.scalar_tensor_tensor(qk_n[:, b].rearrange("p (h d) -> p h d", d=D1),
                                             rnorm[:, b].rearrange("p (h o) -> p h o", o=1)
                                             .broadcast_to([P, 8, D1]), 1e8 / 8,
                                             ps_kq[b][:].rearrange("p (h d) -> p h d", d=D1),
                                             ALU.min, ALU.mult).then_inc(kq_normed, 1)
                ok, jj, kk, g = group(j, k, 13)
                if ok and kk % 4 == 3:
                    t = 2 * jj + kk // 4
                    dve.wait_ge(y_made, t + 1)
                    xt = xres[:, bass.ds(t, 1), :]
                    dve.scalar_tensor_tensor(xt, ps_t[:, 0:P].rearrange("p (o d) -> p o d", o=1),
                                             c["tanhs"][:, 1:2], xt, ALU.mult, ALU.add).then_inc(x_done, 1)
                ok, jj, kk, g = group(j, k, 0)
                if ok and kk % 4 == 0:
                    t, b = 2 * jj + kk // 4, kk // 4
                    if isinstance(t, int):
                        dve.wait_ge(stats_done, 2 * (t + 1))
                    for src in range(2):
                        dve.bn_aggr(mean_var[:, b, src], stats[:, b, src]).then_inc(mv_done, 1)
                    dve.wait_ge(mv_done, 2 * (t + 1))
                    dve.tensor_scalar(var_eps[:, b, 0:1], mean_var[:, b, 0, 1:2], EPS, None,
                                      ALU.add).then_inc(eps_added, 1)
                    dve.tensor_scalar(var_eps[:, b, 1:2], mean_var[:, b, 1, 1:2], 1.0 + EPS, EPS * EPS,
                                      ALU.mult, ALU.add).then_inc(eps_added, 1)
                ok, jj, kk, g = group(j, k, 3)
                for keys in [] if not ok else [False, True] if kk % 2 == 0 else [True]:
                    n, b = use(jj, kk, keys), use(0, kk, keys) % 3
                    dve.wait_ge(squared, n + 1)
                    dve.reduce_sum(square_sums[:, b], squares[:, b].rearrange("p (h d) -> p h d", d=D1),
                                   AX.X).then_inc(reduced, 1)

            turns(dve, body, LAGS, G, UNG)

        @block.tensor
        def _(pe):
            pe.wait_ge(w_in, 16 * NW)
            pe.wait_ge(ready, 4)

            def three(out, sh, sl, mh, ml):
                pe.matmul(out, sh, mh, start=True, stop=False)
                pe.matmul(out, sh, ml, start=False, stop=False)
                return pe.matmul(out, sl, mh, start=False, stop=True)

            def turn_keys(jj, kk, g):
                if kk % 2 == 0:
                    pe.wait_ge(q_copied, 2 * (4 * jj + kk // 2 + 1))
                else:
                    pe.wait_ge(kT_copied, g)
                pe.wait_ge(kq_normed, use(jj, kk, True) + 1)
                for u in range(4):
                    mm = pe.transpose(ps_t[:, u * P:(u + 1) * P],
                                      qk_n[:, 1 + kk % 2, u * P:(u + 1) * P], c["ident"][:])
                mm.then_inc(k_turned, 1)

            def body(j, k):
                ok, jj, kk, g = group(j, k, 5)
                if ok and kk % 2 == 0:
                    pe.wait_ge(kq_normed, use(jj, kk, False) + 1)
                    t = 2 * jj + kk // 4
                    if kk % 4 == 0 and past(t, 3):
                        pe.wait_ge(x_done, t - 2)
                    elif kk % 4 == 2 and not (isinstance(t, int) and t + 1 >= NT):
                        pe.wait_ge(zT_done, 2 * (t + 2))
                    elif past(g, 1):
                        pe.wait_ge(kT_copied, g)
                    for u in range(4):
                        mm = pe.transpose(ps_t[:, u * P:(u + 1) * P], qk_n[:, 0, u * P:(u + 1) * P],
                                          c["ident"][:])
                    mm.then_inc(q_turned, 1)
                if ok and kk % 2 == 1:
                    turn_keys(jj, kk, g)
                ok, jj, kk, g = group(j, k, 7)
                if ok:
                    tb, half, q = kk // 4, (kk // 2) % 2, kk % 2
                    cols = slice(INNER + half * HALF, INNER + (half + 1) * HALF)
                    if past(g, 2):
                        pe.wait_ge(probsT_copied, g - 1)
                    elif past(g, 1):
                        pe.wait_ge(v_copied, g)
                    three(ps_vp[:], keys_h[:, tb, q], keys_l[:, tb, q], wkv_h[:, cols],
                          wkv_l[:, cols]).then_inc(v_made, 1)
                ok, jj, kk, g = group(j, k, 5)
                if ok and kk % 2 == 0:
                    turn_keys(jj, kk, g)
                ok, jj, kk, g = group(j, k, 2)
                if ok and kk % 4 == 0:
                    t, b = 2 * jj + kk // 4, kk // 4
                    pe.wait_ge(z_done, 2 * (t + 1))
                    if past(t, 1):
                        pe.wait_ge(kT_copied, 4 * t - 2)
                    pe.transpose(ps_t[:, 0:P], z[:, b, 0], c["ident"][:])
                    pe.transpose(ps_t[:, P:2 * P], z[:, b, 1], c["ident"][:]).then_inc(z_turned, 1)
                ok, jj, kk, g = group(j, k, 9)
                if ok:
                    b = kk % 2
                    pe.wait_ge(probsT_copied, g + 1)
                    if past(g, 1):
                        pe.wait_ge(o_copied, 2 * g)
                    for u in range(4):
                        mm = pe.matmul(ps_o[:, u * P:(u + 1) * P], v[:, kk % 4, u * P:(u + 1) * P],
                                       probsT[:, b, u], start=True, stop=True)
                    mm.then_inc(o_made, 1)
                ok, jj, kk, g = group(j, k, 13)
                if ok and kk % 4 == 3:
                    t, tb = 2 * jj + kk // 4, kk // 4
                    pe.wait_ge(o_copied, 2 * (g + 1))
                    if isinstance(t, int) and t + 3 > NT:
                        pe.wait_ge(x_done, t)
                    else:
                        pe.wait_ge(kT_copied, 4 * (t + 3))
                    for u in range(H1 // 2):
                        pe.matmul(ps_t[:, 0:P], oT[:, tb, u].rearrange("p q n -> p (q n)"), w_out[:, u, :],
                                  start=(u == 0), stop=False)
                    pe.matmul(ps_t[:, 0:P], c["ones_row"][:], b_out[:], start=False, stop=True).then_inc(y_made, 1)
                ok, jj, kk, g = group(j, k, 3)
                if ok:
                    t, tb, half, q = 2 * jj + kk // 4, kk // 4, (kk // 2) % 2, kk % 2
                    cols = slice(half * HALF, (half + 1) * HALF)
                    if kk % 4 == 0:
                        pe.wait_ge(keys_l_done, t + 1)
                        pe.wait_ge(lat_done, 2 * (t + 1))
                    for keys in ([False, True] if kk % 2 == 0 else [True]):
                        n, b = use(jj, kk, keys), use(0, kk, keys) % 3
                        if past(n, 3):
                            pe.wait_ge(kq_normed, n - 2)
                        if keys:
                            mm = three(ps_kq[b][:], keys_h[:, tb, q], keys_l[:, tb, q], wkv_h[:, cols], wkv_l[:, cols])
                        else:
                            mm = three(ps_kq[b][:], lat_h[:, tb], lat_l[:, tb], wq_h[:, cols], wq_l[:, cols])
                        mm.then_inc(kq_made, 1)
                ok, jj, kk, g = group(j, k, 8)
                if ok:
                    b = kk % 2
                    pe.wait_ge(probs_normed, 4 * (g + 1))
                    pe.wait_ge(v_copied, g + 2 if not isinstance(g, int) else min(g + 2, G))
                    for u in range(4):
                        mm = pe.transpose(ps_vp[:, u * P:(u + 1) * P], probs_n[:, b, u], c["ident"][:])
                    mm.then_inc(probs_turned, 1)
                ok, jj, kk, g = group(j, k, 6)
                if ok:
                    b, tb, hb, q = kk % 2, kk // 4, (kk // 2) % 2, kk % 2
                    if kk % 4 == 0:
                        pe.wait_ge(mask_done, 2 * jj + kk // 4 + 1)
                    if kk % 2 == 0:
                        pe.wait_ge(q_copied, 2 * (4 * jj + kk // 2 + 1))
                    pe.wait_ge(kT_copied, g + 1)
                    if past(g, 2):
                        pe.wait_ge(probs_done, 4 * (g - 1))
                    pe.matmul(ps_s[b][:], ones_b[:], mask_row[:, tb, q:q + 1, :].broadcast_to([1, 4, P]),
                              start=True, stop=True, skip_group_check=True)
                    for u in range(4):
                        mm = pe.matmul(ps_s[b][:, u * P:(u + 1) * P], q_diag[:, hb, u, q], kT[:, b, u],
                                       start=False, stop=True, skip_group_check=True)
                    mm.then_inc(scores_done, 1)

            turns(pe, body, LAGS, G, UNG)


def route(nc, c, xres, a, zT_h, zT_l, weight):
    LAGS = 3
    NE = NT * E
    with ExitStack() as ctx:
        m = Mem(nc, ctx, "route_")
        gateT = m.sb("gateT", [P, E])
        stats = m.sb("r_stats", [P, 2, 6])
        mean_var = m.sb("r_mean_var", [P, 2, 2])
        var_eps = m.sb("r_var_eps", [P, 2, 1])
        rstd = m.sb("r_rstd", [P, 2, 1])
        z = m.sb("r_z", [P, 2, D])
        zT = m.sb("r_zT", [P, 2, P])
        first_key = m.sb("first_key", [P, E])
        logits, keyed, hot1, hot2, rest = (m.sb(n, [P, NT, E]) for n in ("logits", "keyed", "hot1", "hot2", "rest"))
        top1, top2, best, gap, odds, p1, p2 = (
            m.sb(n, [P, NT]) for n in ("top1", "top2", "best", "gap", "odds", "p1", "p2"))
        ps_T = [m.ps("ps_T0"), m.ps("ps_T1")]
        ps_l = [m.ps("ps_l0"), m.ps("ps_l1")]
        names = ("w_in", "keys_made", "stats_done", "mv_done", "eps_added", "rstd_done", "z_done", "z_turned",
                 "zT_copied", "high_done", "low_done", "logits_made", "logits_copied", "chain", "odds_done")
        (w_in, keys_made, stats_done, mv_done, eps_added, rstd_done, z_done, z_turned, zT_copied, high_done,
         low_done, logits_made, logits_copied, chain, odds_done) = (m.sem("r_" + n) for n in names)
        block = ctx.enter_context(nc.Block())

        @block.sync
        def _(sp):
            sp.dma_start(gateT[:], a["L0_ffn_gate_wT"]).then_inc(w_in, 16)

        @block.gpsimd
        def _(pool):
            for e in range(E):
                pool.memset(first_key[:, e:e + 1], float(E - e)).then_inc(keys_made, 1)

            def body(s, k):
                if live(s, 0):
                    b = k % 2
                    pool.wait_ge(eps_added, s + 1)
                    pool.tensor_tensor(rstd[:, b, :], var_eps[:, b, :], c["half_pow"][:, 0:1],
                                       ALU.pow).then_inc(rstd_done, 1)
                if live(s, 2):
                    t, b = s - 2, (k - 2) % 2
                    pool.wait_ge(high_done, t + 1)
                    pool.tensor_tensor(zT_l[:, bass.ds(t, 1), :], zT[:, b:b + 1, :],
                                       zT_h[:, bass.ds(t, 1), :], ALU.subtract).then_inc(low_done, 1)

            slots(pool, body, LAGS)

        @block.scalar
        def _(act):
            def body(s, k):
                if live(s, 1):
                    t, b = s - 1, (k - 1) % 2
                    act.wait_ge(z_turned, t + 1)
                    if since(t, 2):
                        act.wait_ge(low_done, t - 1)
                        act.wait_ge(logits_made, t - 1)
                    act.copy(zT[:, b, :], ps_T[b][:, 0:P]).then_inc(zT_copied, 1)
                    act.wait_ge(zT_copied, t + 1)
                    act.copy(zT_h[:, bass.ds(t, 1), :], zT[:, b:b + 1, :]).then_inc(high_done, 1)

            slots(act, body, LAGS)
            act.wait_ge(chain, 12)
            act.activation(odds[:], gap[:], ACT.Exp).then_inc(odds_done, 1)

        @block.tensor
        def _(pe):
            pe.wait_ge(w_in, 16)

            def body(s, k):
                if live(s, 1):
                    t, b = s - 1, (k - 1) % 2
                    pe.wait_ge(z_done, t + 1)
                    if since(t, 2):
                        pe.wait_ge(zT_copied, t - 1)
                    pe.transpose(ps_T[b][:, 0:P], z[:, b, :], c["ident"][:]).then_inc(z_turned, 1)
                if live(s, 2):
                    t, b = s - 2, (k - 2) % 2
                    pe.wait_ge(zT_copied, t + 1)
                    if since(t, 2):
                        pe.wait_ge(logits_copied, t - 1)
                    pe.matmul(ps_l[b][:, 0:E], zT[:, b, :], gateT[:], start=True, stop=True).then_inc(logits_made, 1)

            slots(pe, body, LAGS)

        @block.vector
        def _(dve):
            def body(s, k):
                if live(s, 1):
                    t, b = s - 1, (k - 1) % 2
                    dve.wait_ge(rstd_done, t + 1)
                    if since(t, 2):
                        dve.wait_ge(z_turned, t - 1)
                    dve.tensor_scalar(z[:, b, :], xres[:, bass.ds(t, 1), :].rearrange("p o d -> p (o d)"),
                                      mean_var[:, b, 0:1], rstd[:, b, :],
                                      ALU.subtract, ALU.mult).then_inc(z_done, 1)
                if live(s, 0):
                    b = k % 2
                    b0 = k % 2
                    dve.bn_stats(stats[:, b0, :], xres[:, bass.ds(s, 1), :]).then_inc(stats_done, 1)
                if live(s, 3):
                    t, b = s - 3, (k - 3) % 2
                    if live(s, 0):
                        dve.wait_ge(stats_done, s + 1)
                    dve.wait_ge(logits_made, t + 1)
                    dve.tensor_copy(logits[:, bass.ds(t, 1), :],
                                    ps_l[b][:, 0:E].rearrange("p (o e) -> p o e", o=1)).then_inc(logits_copied, 1)

                if live(s, 0):
                    if isinstance(s, int):
                        dve.wait_ge(stats_done, s + 1)
                    dve.bn_aggr(mean_var[:, b0, :], stats[:, b0, :]).then_inc(mv_done, 1)
                    dve.wait_ge(mv_done, s + 1)
                    dve.tensor_scalar(var_eps[:, b0, :], mean_var[:, b0, 1:2], EPS, None,
                                      ALU.add).then_inc(eps_added, 1)

            slots(dve, body, LAGS)
            dve.wait_ge(logits_copied, NT)
            dve.wait_ge(keys_made, E)

            def wide(v):
                return v.rearrange("p (t o) -> p t o", o=1).broadcast_to([P, NT, E])

            done = [0]

            def then(ins):
                done[0] += 1
                ins.then_inc(chain, 1)
                dve.wait_ge(chain, done[0])

            keys = first_key[:].rearrange("p (o e) -> p o e", o=1).broadcast_to([P, NT, E])
            for src, top, hot in ((logits, top1, hot1), (rest, top2, hot2)):
                then(dve.tensor_reduce(top[:], src[:], AX.X, ALU.max))
                then(dve.tensor_tensor(keyed[:], src[:], wide(top[:]), ALU.is_equal))
                then(dve.tensor_tensor(keyed[:], keyed[:], keys, ALU.mult))
                then(dve.tensor_reduce(best[:], keyed[:], AX.X, ALU.max))
                then(dve.tensor_tensor(hot[:], keyed[:], wide(best[:]), ALU.is_equal))
                if src is logits:
                    then(dve.scalar_tensor_tensor(rest[:].rearrange("p t e -> p (t e)"),
                                                  hot1[:].rearrange("p t e -> p (t e)"), -3e38,
                                                  logits[:].rearrange("p t e -> p (t e)"), ALU.mult, ALU.add))
            then(dve.tensor_tensor(gap[:], top2[:], top1[:], ALU.subtract))
            dve.wait_ge(odds_done, 1)
            then(dve.tensor_scalar(p2[:], odds[:], 1.0, None, ALU.add))
            then(dve.reciprocal(p1[:], p2[:]))
            then(dve.tensor_scalar(p1[:], p1[:], c["tanhs"][:, 2:3], None, ALU.mult))
            then(dve.tensor_tensor(p2[:], p1[:], odds[:], ALU.mult))
            then(dve.tensor_tensor(hot1[:], hot1[:], wide(p1[:]), ALU.mult))
            then(dve.tensor_tensor(hot2[:], hot2[:], wide(p2[:]), ALU.mult))
            then(dve.tensor_tensor(weight[:], hot1[:], hot2[:], ALU.add))


def experts(nc, c, xres, a):
    UNIT, T4, LAGS = E, 4, 1
    CH = I // P
    with ExitStack() as ctx:
        m = Mem(nc, ctx, "moe_")
        zT_h, zT_l = (m.sb(n, [P, NT, P], BF16) for n in ("zT_h", "zT_l"))
        weight = m.sb("weight", [P, NT, E])
        route(nc, c, xres, a, zT_h, zT_l, weight)
        wg_h, wg_l, wu_h, wu_l, wd_h, wd_l = (m.sb(n, [P, E * I], BF16) for n in (
            "wg_h", "wg_l", "wu_h", "wu_l", "wd_h", "wd_l"))
        split_weights(nc, "b", m, [
            (hi, lo, [(slice(e * I, (e + 1) * I), a[n][e]) for e in range(E)])
            for hi, lo, n in ((wg_h, wg_l, "L0_ffn_wgT"), (wu_h, wu_l, "L0_ffn_wuT"), (wd_h, wd_l, "L0_ffn_wdT"))])
        gate = m.sb("gate", [P, 2, 512])
        hid = m.sb("hid", [P, 2, 512])
        hid_h, hid_l = (m.sb(n, [P, 2, CH, 512], BF16) for n in ("hid_h", "hid_l"))
        ps_g, ps_u, ps_d = ([m.ps(f"ps_{n}{i}") for i in range(2)] for n in "gud")
        names = ("gate_made", "up_made", "silu_done", "hid_done", "high_done", "low_done", "down_made", "x_done")
        gate_made, up_made, silu_done, hid_done, high_done, low_done, down_made, x_done = (
            m.sem("b_" + n) for n in names)
        block = ctx.enter_context(nc.Block())
        NG = NT // T4
        N = NG * E

        def unit(j, e, lag):
            j, e = at(j, e, lag, E)
            n = j * E + e
            return not isinstance(n, int) or 0 <= n < N, j, e, n

        def past(x, least):
            return not isinstance(x, int) or x >= least

        @block.tensor
        def _(pe):
            def body(j, k):
                for i in range(CH):
                    ok, g, e, n = unit(j, k, 0)
                    if ok:
                        b = i % 2
                        cols = slice(e * I + i * P, e * I + (i + 1) * P)
                        zh = zT_h[:, bass.ds(g * T4, T4), :]
                        zl = zT_l[:, bass.ds(g * T4, T4), :]
                        for w_h, w_l, out, made, used in ((wg_h, wg_l, ps_g[b], gate_made, silu_done),
                                                         (wu_h, wu_l, ps_u[b], up_made, hid_done)):
                            if past(CH * n + i, 2):
                                pe.wait_ge(used, CH * n + i - 1)
                            pe.matmul(out[:], w_h[:, cols], zh, start=True, stop=False)
                            pe.matmul(out[:], w_h[:, cols], zl, start=False, stop=False)
                            pe.matmul(out[:], w_l[:, cols], zh, start=False, stop=True).then_inc(made, 1)
                    ok, g, e, n = unit(j, k, 1)
                    if ok:
                        b = e % 2
                        if i == 0 and past(n, 2):
                            pe.wait_ge(x_done, T4 * (n - 1))
                        pe.wait_ge(low_done, CH * n + i + 1)
                        cols = slice(e * I + i * P, e * I + (i + 1) * P)
                        for t in range(T4):
                            rows_ = slice(t * P, (t + 1) * P)
                            for p, (h, w) in enumerate(((hid_h, wd_h), (hid_h, wd_l), (hid_l, wd_h))):
                                mm = pe.matmul(ps_d[b][:, rows_], h[:, b, i, rows_], w[:, cols],
                                               start=(i == 0 and t == 0 and p == 0), stop=(i == CH - 1 and p == 2),
                                               skip_group_check=True)
                        if i == CH - 1:
                            mm.then_inc(down_made, 1)

            turns(pe, body, LAGS, N, E)

        @block.scalar
        def _(act):
            def body(j, k):
                ok, g, e, n = unit(j, k, 0)
                if not ok:
                    return
                for i in range(CH):
                    b, q = i % 2, CH * n + i
                    act.wait_ge(gate_made, q + 1)
                    if past(q, 2):
                        act.wait_ge(hid_done, q - 1)
                    act.activation(gate[:, b], ps_g[b][:], ACT.Silu).then_inc(silu_done, 1)
                    if i >= 1:
                        high(act, n, e, i - 1)
                high(act, n, e, CH - 1)

            def high(act, n, e, i):
                q = CH * n + i
                act.wait_ge(hid_done, q + 1)
                if i == 0 and past(n, 2):
                    act.wait_ge(down_made, n - 1)
                act.copy(hid_h[:, e % 2, i], hid[:, i % 2]).then_inc(high_done, 1)

            turns(act, body, LAGS, N, E)

        @block.vector
        def _(dve):
            def low(n, e, i):
                q = CH * n + i
                dve.wait_ge(high_done, q + 1)
                dve.tensor_tensor(hid_l[:, e % 2, i], hid[:, i % 2], hid_h[:, e % 2, i],
                                  ALU.subtract).then_inc(low_done, 1)

            def body(j, k):
                ok, g, e, n = unit(j, k, 0)
                if ok:
                    for i in range(CH):
                        b, q = i % 2, CH * n + i
                        dve.wait_ge(silu_done, q + 1)
                        dve.wait_ge(up_made, q + 1)
                        if i == 0 and past(n, 2):
                            dve.wait_ge(down_made, n - 1)
                        if past(q, 2):
                            dve.wait_ge(low_done, q - 1)
                        dve.tensor_tensor(hid[:, b], gate[:, b], ps_u[b][:], ALU.mult).then_inc(hid_done, 1)
                        if i >= 1:
                            low(n, e, i - 1)
                    low(n, e, CH - 1)
                ok, g, e, n = unit(j, k, 1)
                if ok:
                    dve.wait_ge(down_made, n + 1)
                    for t in range(T4):
                        if past(n, 1):
                            dve.wait_ge(x_done, T4 * (n - 1) + t + 1)
                        xt = xres[:, bass.ds(g * T4 + t, 1), :].rearrange("p o d -> p (o d)")
                        wt = weight[:, bass.ds(g * T4 + t, 1), e]
                        dve.scalar_tensor_tensor(xt, ps_d[e % 2][:, t * P:(t + 1) * P], wt, xt,
                                                 ALU.mult, ALU.add).then_inc(x_done, 1)

            turns(dve, body, LAGS, N, E)


def ternary(nc, c, xres, a):
    LAGS = 6
    LEVELS = 127.0
    CH = HID // P
    with ExitStack() as ctx:
        m = Mem(nc, ctx, "tern_")
        raw = m.sb("q_raw", [P, 3, HID])
        rounded = m.sb("q_rounded", [P, 3, HID])
        w = m.sb("w_ternary", [P, 3, HID], BF16)
        ones = m.sb("ones", [P, P])
        part = m.sb("part", [P, 3])
        mean = m.sb("mean", [P, 3])
        wscale = m.sb("wscale", [P, 3])
        stats = m.sb("q_stats", [P, 2, 6])
        mean_var = m.sb("q_mean_var", [P, 2, 2])
        var_eps = m.sb("q_var_eps", [P, 2, 1])
        rstd = m.sb("q_rstd", [P, 2, 1])
        z = m.sb("q_z", [P, 2, D])
        size = m.sb("size", [P, 2, 1])
        unit_ = m.sb("unit", [P, 2, 1])
        scale = m.sb("scale", [P, 2, 1])
        back = m.sb("back", [P, UN, 2])
        xr = m.sb("xr", [P, 2, D])
        xq = m.sb("xq", [P, 2, D], BF16)
        xqT = m.sb("xqT", [P, 2, P], BF16)
        gate = m.sb("q_gate", [P, 2, HID])
        hid = m.sb("q_hid", [P, 2, HID])
        hsize = m.sb("hsize", [P, 2, 1])
        hunit = m.sb("hunit", [P, 2, 1])
        hscale = m.sb("hscale", [P, 2, 1])
        hback = m.sb("hback", [P, UN, 1])
        hr = m.sb("hr", [P, 2, HID])
        hq = m.sb("hq", [P, 2, HID], BF16)
        hqT = m.sb("hqT", [P, 2, CH, P], BF16)
        ps_x, ps_h, ps_y, ps_m = (m.ps(n) for n in ("ps_x", "ps_h", "ps_y", "ps_m"))
        ps_g, ps_u = ([m.ps(f"ps_{n}{i}") for i in range(2)] for n in "gu")
        names = ("stats_done", "mv_done", "eps_added", "rstd_done", "z_done", "w_in", "ones_made", "chain", "summed", "w_done", "size_done", "unit_done", "scale_done",
                 "back_done", "xr_done", "xq_done", "x_turned", "xqT_copied", "gu_made", "gate_done", "hid_done",
                 "hsize_done", "hunit_done", "hscale_done", "hback_done", "hr_done", "hq_done", "h_turned",
                 "hqT_copied", "y_made", "x_done")
        (stats_done, mv_done, eps_added, rstd_done, z_done, w_in, ones_made, chain, summed, w_done, size_done, unit_done, scale_done, back_done, xr_done, xq_done,
         x_turned, xqT_copied, gu_made, gate_done, hid_done, hsize_done, hunit_done, hscale_done, hback_done,
         hr_done, hq_done, h_turned, hqT_copied, y_made, x_done) = (m.sem("d_" + n) for n in names)
        block = ctx.enter_context(nc.Block())

        @block.sync
        def _(sp):
            for n, name in enumerate(("w_gateT", "w_upT", "w_downT")):
                sp.dma_start(raw[:, n, :], a["L1_ffn_" + name]).then_inc(w_in, 16)

        @block.gpsimd
        def _(pool):
            pool.memset(ones[:], 1.0).then_inc(ones_made, 1)

            def body(s, k):
                if live(s, 0):
                    b = k % 2
                    pool.wait_ge(eps_added, s + 1)
                    pool.tensor_tensor(rstd[:, b, :], var_eps[:, b, :], c["half_pow"][:, 0:1],
                                       ALU.pow).then_inc(rstd_done, 1)
                if live(s, 1):
                    t, b, kt = s - 1, (k - 1) % 2, (k - 1) % UN
                    pool.wait_ge(unit_done, t + 1)
                    pool.wait_ge(w_done, 1)
                    if since(t, 4):
                        pool.wait_ge(hid_done, t - 3)
                    pool.tensor_tensor(back[:, kt, :], unit_[:, b, :].broadcast_to([P, 2]), mean[:, 0:2],
                                       ALU.mult).then_inc(back_done, 1)
                if live(s, 4):
                    t, b, kt = s - 4, (k - 4) % 2, (k - 4) % UN
                    pool.wait_ge(hunit_done, t + 1)
                    if since(t, 4):
                        pool.wait_ge(x_done, t - 3)
                    pool.tensor_tensor(hback[:, kt, :], hunit[:, b, :], mean[:, 2:3],
                                       ALU.mult).then_inc(hback_done, 1)

            slots(pool, body, LAGS)

        @block.scalar
        def _(act):
            def body(s, k):
                if live(s, 2):
                    t, b = s - 2, (k - 2) % 2
                    act.wait_ge(x_turned, t + 1)
                    if since(t, 2):
                        act.wait_ge(gu_made, 2 * (t - 1))
                    act.copy(xqT[:, b, :], ps_x[:].bitcast(BF16)[:, 0:P]).then_inc(xqT_copied, 1)
                if live(s, 5):
                    t, b = s - 5, (k - 5) % 2
                    act.wait_ge(h_turned, t + 1)
                    if since(t, 2):
                        act.wait_ge(y_made, t - 1)
                    act.copy(hqT[:, b].rearrange("p c n -> p (c n)"),
                             ps_h[:].bitcast(BF16)[:, 0:HID]).then_inc(hqT_copied, 1)
                if live(s, 3):
                    t, b, kt = s - 3, (k - 3) % 2, (k - 3) % UN
                    act.wait_ge(gu_made, 2 * t + 1)
                    act.wait_ge(back_done, t + 1)
                    if since(t, 2):
                        act.wait_ge(hid_done, t - 1)
                    act.activation(gate[:, b], ps_g[b][:], ACT.Silu, scale=back[:, kt, 0:1]).then_inc(gate_done, 1)

            slots(act, body, LAGS)

        @block.tensor
        def _(pe):
            pe.wait_ge(chain, 1)
            pe.wait_ge(ones_made, 1)
            pe.matmul(ps_m[:, 0:3], ones[:], part[:], start=True, stop=True).then_inc(summed, 1)
            pe.wait_ge(w_done, 1)

            def body(s, k):
                if live(s, 6):
                    t, b = s - 6, (k - 6) % 2
                    pe.wait_ge(hqT_copied, t + 1)
                    if since(t, 1):
                        pe.wait_ge(x_done, t)
                    for i in range(CH):
                        mm = pe.matmul(ps_y[:, 0:P], hqT[:, b, i, :], w[:, 2, i * P:(i + 1) * P],
                                       start=(i == 0), stop=(i == CH - 1))
                    mm.then_inc(y_made, 1)
                if live(s, 3):
                    t, b = s - 3, (k - 3) % 2
                    pe.wait_ge(xqT_copied, t + 1)
                    for i, (out, used) in enumerate(((ps_g[b], gate_done), (ps_u[b], hid_done))):
                        if since(t, 2):
                            pe.wait_ge(used, t - 1)
                        pe.matmul(out[:], xqT[:, b, :], w[:, i, :], start=True, stop=True).then_inc(gu_made, 1)
                if live(s, 2):
                    t, b = s - 2, (k - 2) % 2
                    pe.wait_ge(xq_done, t + 1)
                    if since(t, 1):
                        pe.wait_ge(xqT_copied, t)
                    pe.transpose(ps_x[:].bitcast(BF16)[:, 0:P], xq[:, b, :], c["ident_b"][:]).then_inc(x_turned, 1)
                if live(s, 5):
                    t, b = s - 5, (k - 5) % 2
                    pe.wait_ge(hq_done, t + 1)
                    if since(t, 1):
                        pe.wait_ge(hqT_copied, t)
                    for i in range(CH):
                        mm = pe.transpose(ps_h[:].bitcast(BF16)[:, i * P:(i + 1) * P], hq[:, b, i * P:(i + 1) * P],
                                          c["ident_b"][:])
                    mm.then_inc(h_turned, 1)

            slots(pe, body, LAGS)

        @block.vector
        def _(dve):
            dve.wait_ge(w_in, 48)
            dve.tensor_reduce(part[:], raw[:], AX.X, ALU.add, apply_absolute_value=True).then_inc(chain, 1)
            dve.wait_ge(summed, 1)
            dve.tensor_scalar(mean[:], ps_m[:, 0:3], 1.0 / (D * HID), 1e-5, ALU.mult, ALU.max).then_inc(chain, 1)
            dve.wait_ge(chain, 2)
            dve.reciprocal(wscale[:], mean[:]).then_inc(chain, 1)
            dve.wait_ge(chain, 3)
            for n in range(3):
                dve.tensor_scalar(rounded[:, n], raw[:, n], wscale[:, n:n + 1], ROUND,
                                  ALU.mult, ALU.add).then_inc(chain, 1)
            dve.wait_ge(chain, 6)
            dve.tensor_scalar(rounded[:], rounded[:], ROUND, 1.0, ALU.subtract, ALU.min).then_inc(chain, 1)
            dve.wait_ge(chain, 7)
            dve.tensor_scalar(w[:], rounded[:], -1.0, None, ALU.max).then_inc(w_done, 1)
            dve.tensor_scalar(mean[:, 2:3], mean[:, 2:3], c["tanhs"][:, 3:4], None, ALU.mult).then_inc(w_done, 1)

            def body(s, k):
                hid_on, x_on = live(s, 4), live(s, 1)
                t, b, kt = s - 4, (k - 4) % 2, (k - 4) % UN
                n, bn = s - 1, (k - 1) % 2
                if hid_on:
                    dve.wait_ge(gate_done, t + 1)
                    dve.wait_ge(gu_made, 2 * (t + 1))
                    dve.scalar_tensor_tensor(hid[:, b], ps_u[b][:], back[:, kt, 1:2], gate[:, b],
                                             ALU.mult, ALU.mult).then_inc(hid_done, 1)
                if x_on:
                    xt = xres[:, bass.ds(n, 1), :].rearrange("p o d -> p (o d)")
                    dve.wait_ge(rstd_done, n + 1)
                    dve.tensor_scalar(z[:, bn, :], xt, mean_var[:, bn, 0:1], rstd[:, bn, :],
                                      ALU.subtract, ALU.mult).then_inc(z_done, 1)
                if hid_on:
                    dve.wait_ge(hid_done, t + 1)
                    dve.tensor_reduce(hsize[:, b], hid[:, b], AX.X, ALU.max,
                                      apply_absolute_value=True).then_inc(hsize_done, 1)
                if x_on:
                    dve.wait_ge(z_done, n + 1)
                    dve.tensor_reduce(size[:, bn], z[:, bn, :], AX.X, ALU.max,
                                      apply_absolute_value=True).then_inc(size_done, 1)
                if hid_on:
                    dve.wait_ge(hsize_done, t + 1)
                    if since(t, 2):
                        dve.wait_ge(hback_done, t - 1)
                    dve.tensor_scalar(hunit[:, b], hsize[:, b], 1e-5, 1.0 / LEVELS, ALU.max, ALU.mult).then_inc(hunit_done, 1)
                if x_on:
                    dve.wait_ge(size_done, n + 1)
                    if since(n, 2):
                        dve.wait_ge(back_done, n - 1)
                    dve.tensor_scalar(unit_[:, bn], size[:, bn], 1e-5, 1.0 / LEVELS, ALU.max, ALU.mult).then_inc(unit_done, 1)
                if hid_on:
                    dve.wait_ge(hunit_done, t + 1)
                    dve.reciprocal(hscale[:, b], hunit[:, b]).then_inc(hscale_done, 1)
                if x_on:
                    dve.wait_ge(unit_done, n + 1)
                    dve.reciprocal(scale[:, bn], unit_[:, bn]).then_inc(scale_done, 1)
                if hid_on:
                    dve.wait_ge(hscale_done, t + 1)
                    dve.tensor_scalar(hr[:, b], hid[:, b], hscale[:, b], ROUND, ALU.mult, ALU.add).then_inc(hr_done, 1)
                if x_on:
                    dve.wait_ge(scale_done, n + 1)
                    dve.tensor_scalar(xr[:, bn], z[:, bn, :], scale[:, bn], ROUND, ALU.mult, ALU.add).then_inc(xr_done, 1)
                if hid_on:
                    dve.wait_ge(hr_done, t + 1)
                    if since(t, 2):
                        dve.wait_ge(h_turned, t - 1)
                    dve.tensor_scalar(hq[:, b], hr[:, b], ROUND, LEVELS, ALU.subtract, ALU.min).then_inc(hq_done, 1)
                if x_on:
                    dve.wait_ge(xr_done, n + 1)
                    if since(n, 2):
                        dve.wait_ge(x_turned, n - 1)
                    dve.tensor_scalar(xq[:, bn], xr[:, bn], ROUND, LEVELS, ALU.subtract, ALU.min).then_inc(xq_done, 1)
                if live(s, 0):
                    b0 = k % 2
                    dve.bn_stats(stats[:, b0, :], xres[:, bass.ds(s, 1), :]).then_inc(stats_done, 1)
                if live(s, 6):
                    t, kt = s - 6, (k - 6) % UN
                    if live(s, 0):
                        dve.wait_ge(stats_done, s + 1)
                    dve.wait_ge(y_made, t + 1)
                    dve.wait_ge(hback_done, t + 1)
                    xt = xres[:, bass.ds(t, 1), :].rearrange("p o d -> p (o d)")
                    dve.scalar_tensor_tensor(xt, ps_y[:, 0:P], hback[:, kt, :], xt, ALU.mult, ALU.add).then_inc(x_done, 1)

                if live(s, 0):
                    if isinstance(s, int):
                        dve.wait_ge(stats_done, s + 1)
                    dve.bn_aggr(mean_var[:, b0, :], stats[:, b0, :]).then_inc(mv_done, 1)
                    dve.wait_ge(mv_done, s + 1)
                    dve.tensor_scalar(var_eps[:, b0, :], mean_var[:, b0, 1:2], EPS, None,
                                      ALU.add).then_inc(eps_added, 1)

            slots(dve, body, LAGS)


def build(nc, out, a):
    with ExitStack() as ctx:
        m = Mem(nc, ctx)
        xres = m.sb("xres", [P, NT, D])
        c = setup(nc, m, a)
        load_x(nc, xres, a)
        causal_attention(nc, c, xres, a)
        experts(nc, c, xres, a)
        perceiver(nc, c, xres, a)
        ternary(nc, c, xres, a)
        store_x(nc, xres, out)


def layouts(i):
    import numpy as np

    def chunks(w):
        out, inner = w.shape
        return w.T.reshape(inner // P, P, out).transpose(1, 0, 2).reshape(P, -1)

    a = {"x": i["x"].reshape(NT, P, D), "ctx": i["ctx_1024"].reshape(NT, P, D),
         "mask": i["mask_BxS2_bf1"].view(np.uint8), "g_xattn": i["g_xattn"], "g_ffn": i["g_ffn"]}
    for n in ("wq", "wk", "wv", "wo"):
        a[f"L0_xattn_{n}T"] = i[f"L0_xattn_{n}"].T
    for n in ("bq", "bk", "bv", "bo"):
        a[f"L0_xattn_{n}"] = i[f"L0_xattn_{n}"]
    a["L0_ffn_gate_wT"] = i["L0_ffn_gate_w"].T
    for n in ("wg", "wu"):
        a[f"L0_ffn_{n}T"] = i[f"L0_ffn_{n}"].transpose(0, 2, 1)
    a["L0_ffn_wdT"] = np.stack([chunks(w) for w in i["L0_ffn_wd"]])
    for n in ("ln_x_g", "ln_x_b", "ln_l_g", "ln_l_b", "qn_g", "kn_g", "Wq", "Wkv", "Wout", "bout"):
        a[f"L1_xattn_{n}"] = i[f"L1_xattn_{n}"]
    for n in ("w_gate", "w_up"):
        a[f"L1_ffn_{n}T"] = i[f"L1_ffn_{n}"].T
    a["L1_ffn_w_downT"] = chunks(i["L1_ffn_w_down"])
    return {n: np.ascontiguousarray(v) for n, v in a.items()}


def kernel(**inputs):
    import numpy as np
    import concourse.bacc as bacc
    from concourse.bass_utils import run_bass_kernel_spmd

    nc = bacc.Bacc("TRN2", target_bir_lowering=False, num_devices=1)
    arrays = layouts({n: np.asarray(v) for n, v in inputs.items()})
    a = {n: nc.dram_tensor(n, v.shape, mybir.dt.from_np(v.dtype), kind="ExternalInput").ap()
         for n, v in arrays.items()}
    out = nc.dram_tensor("out", (NT, P, D), F32, kind="ExternalOutput").ap()
    build(nc, out, a)
    r = run_bass_kernel_spmd(nc, [arrays], core_ids=[0])
    return r.results[0]["out"].reshape(B, S, D)
```

```python
from contextlib import ExitStack

import concourse.bass as bass
from concourse import mybir

P = 128
B, S, D = 128, 64, 128
NT = B * S // P
UN = 4
EPS = 1e-5
H0, D0 = 16, 8
E, I = 8, 512
H1, D1 = 16, 64
INNER = H1 * D1
HID = 512
W_GATE, W_UP, W_DOWN, W_Q, W_KV = 0, E * I, 2 * E * I, 3 * E * I, 3 * E * I + INNER
W_ALL = W_KV + 2 * INNER
FAR = -1e30
ROUND = 12582912.0

F32 = mybir.dt.float32
BF16 = mybir.dt.bfloat16
U8 = mybir.dt.uint8
U32 = mybir.dt.uint32
ALU = mybir.AluOpType
ACT = mybir.ActivationFunctionType
AX = mybir.AxisListType


def live(s, lag, count=NT):
    return not isinstance(s, int) or 0 <= s - lag < count


def since(s, lag):
    return not isinstance(s, int) or s >= lag


def slots(eng, body, lags, count=NT, un=UN):
    step = 2 * un
    first = -(-(lags + 2) // step)
    for s in range(first * step):
        body(s, s % un)
    with eng.Fori(first, count // step) as j:
        for k in range(step):
            body(j * step + k, k % un)
    for s in range(count, count + lags):
        body(s, s % un)


def turn(t, k, un=UN):
    return (t - k) * (16 // un) + 16


class Mem:

    def __init__(self, nc, ctx, stage=""):
        self.nc, self.ctx, self.stage = nc, ctx, stage

    def sb(self, name, shape, dt=F32):
        return self.ctx.enter_context(self.nc.sbuf_tensor(self.stage + name, shape, dt))

    def ps(self, name):
        return self.ctx.enter_context(self.nc.psum_tensor(self.stage + name, [P, 512], F32))

    def sem(self, name):
        return self.ctx.enter_context(self.nc.semaphore(name))


def rows(ap, k=P):
    return ap.rearrange("(a n) -> a n", a=1).partition_broadcast(k)


def setup(nc, m, a):
    ident = m.sb("ident", [P, P])
    ident_b = m.sb("ident_b", [P, P], BF16)
    causal = m.sb("causal", [P, S], BF16)
    head_mask = m.sb("head_mask", [P, H0])
    half_pow = m.sb("half_pow", [P, 16])
    ones_row = m.sb("ones_row", [1, P])
    gates = m.sb("gates", [P, 4])
    tanhs = m.sb("tanhs", [P, 4])
    with ExitStack() as ctx:
        t = Mem(nc, ctx)
        filled, picked, gates_in = t.sem("filled"), t.sem("picked"), t.sem("gates_in")
        block = ctx.enter_context(nc.Block())

        @block.sync
        def _(sp):
            sp.dma_start(gates[:, 0:2], rows(a["g_xattn"])).then_inc(gates_in, 16)
            sp.dma_start(gates[:, 2:4], rows(a["g_ffn"])).then_inc(gates_in, 16)

        @block.gpsimd
        def _(pool):
            pool.memset(ident[:], 0.0).then_inc(filled, 1)
            pool.memset(ident_b[:], 0.0).then_inc(filled, 1)
            pool.memset(causal[:], 0.0).then_inc(filled, 1)
            pool.memset(head_mask[:], 1.0).then_inc(filled, 1)
            pool.memset(half_pow[:], -0.5).then_inc(filled, 1)
            pool.memset(ones_row[:], 1.0).then_inc(filled, 1)
            pool.wait_ge(filled, 6)
            pool.affine_select(out=ident[:], in_=ident[:], compare_op=ALU.not_equal, fill=1.0,
                               base=0, pattern=[[-1, P]], channel_multiplier=1).then_inc(picked, 1)
            pool.affine_select(out=ident_b[:], in_=ident_b[:], compare_op=ALU.not_equal, fill=1.0,
                               base=0, pattern=[[-1, P]], channel_multiplier=1).then_inc(picked, 1)
            for h in range(2):
                c = causal[h * S:(h + 1) * S, :]
                pool.wait_ge(picked, 2 + h)
                pool.affine_select(out=c, in_=c, compare_op=ALU.is_ge, fill=FAR, base=0,
                                   pattern=[[-1, S]], channel_multiplier=1).then_inc(picked, 1)
            pool.wait_ge(picked, 4)
            pool.affine_select(out=head_mask[:], in_=head_mask[:], compare_op=ALU.is_ge, fill=0.0,
                               base=0, pattern=[[-D0, H0]], channel_multiplier=1).then_inc(picked, 1)
            pool.wait_ge(picked, 5)
            pool.affine_select(out=head_mask[:], in_=head_mask[:], compare_op=ALU.is_ge, fill=0.0,
                               base=D0 - 1, pattern=[[D0, H0]], channel_multiplier=-1).then_inc(picked, 1)

        @block.scalar
        def _(act):
            act.wait_ge(gates_in, 32)
            act.activation(tanhs[:], gates[:], ACT.Tanh)

    return dict(ident=ident, ident_b=ident_b, causal=causal, head_mask=head_mask,
                half_pow=half_pow, ones_row=ones_row, tanhs=tanhs)


def causal_attention(nc, c, xres, a, zT_h, zT_l, logits, w_h, w_l):
    LAGS = 11
    PART = W_ALL // NT
    with ExitStack() as ctx:
        m = Mem(nc, ctx, "attn_")
        wqT, wkT, wvT, woT = (m.sb(n, [P, D]) for n in ("wqT", "wkT", "wvT", "woT"))
        bq, bk = m.sb("bq", [P, 1]), m.sb("bk", [P, 1])
        bv, bo = m.sb("bv", [P, 1]), m.sb("bo", [1, D])
        b_out = m.sb("b_all", [1, D])
        context = m.sb("context", [P, UN, D])
        stats = m.sb("stats", [P, 2, 6])
        mean_var = m.sb("mean_var", [P, 2, 2])
        var_eps = m.sb("var_eps", [P, 2, 1])
        rstd = m.sb("rstd", [P, 2, 1])
        z = m.sb("z", [P, 2, D])
        xT = m.sb("xT", [P, 2, P])
        cT = m.sb("cT", [P, 2, 2, 2, S])
        qT = m.sb("qT", [P, UN, P])
        kT = m.sb("kT", [P, 2, P])
        k_wide = m.sb("k_wide", [P, 2, H0, P])
        v_wide = m.sb("v_wide", [P, UN, 2, H0 // 2, 2 * D0 + 2])
        peak = m.sb("peak", [P, 2, H0])
        below = m.sb("below", [P, 2, H0, S])
        probs = m.sb("probs", [P, 2, H0, S])
        probsT = m.sb("probsT", [P, 2, 8, P])
        rsum = m.sb("rsum", [P, 2, H0])
        o = m.sb("o", [P, 2, D])
        oT = m.sb("oT", [P, 2, P])
        gateT = m.sb("gateT", [P, E])
        raw = m.sb("raw", [P, UN, PART])
        stats2 = m.sb("r_stats", [P, 2, 6])
        mean_var2 = m.sb("r_mean_var", [P, UN, 2])
        var_eps2 = m.sb("r_var_eps", [P, 2, 1])
        rstd2 = m.sb("r_rstd", [P, UN, 1])
        z2 = m.sb("r_z", [P, 2, D])
        zT = m.sb("r_zT", [P, UN, P])

        ps_T, ps_qkv, ps_o, ps_out = (m.ps(n) for n in ("ps_T", "ps_qkv", "ps_o", "ps_out"))
        ps_s = [m.ps("ps_s0"), m.ps("ps_s1")]
        ps_pT = [m.ps("ps_pT0"), m.ps("ps_pT1")]
        o_ps = ps_o[:, 0:8 * 18].rearrange("p (c w) -> p c w", w=18)

        w_in = m.sem("a_w_in")
        x_first_in, x_in = m.sem("a_x_first_in"), m.sem("a_x_in")
        FIRST, PARTS = 8, 7
        context_in = [m.sem(f"a_context_in{k}") for k in range(UN)]
        bv_turned, b_out_done = m.sem("a_bv_turned"), m.sem("a_b_out_done")
        raw_in = [m.sem(f"a_raw_in{k}") for k in range(UN)]
        (w_high_done, w_low_done, stats2_done, mv2_done, eps2_added, rstd2_done, z2_done, z2_turned,
         z2_copied, high_done, low_done, logits_made, logits_copied) = (m.sem("a_" + n) for n in (
            "w_high_done", "w_low_done", "stats2_done", "mv2_done", "eps2_added", "rstd2_done", "z2_done",
            "z2_turned", "z2_copied", "high_done", "low_done", "logits_made", "logits_copied"))
        (v_cleared, stats_done, mv_done, eps_added, rstd_done, z_done, xc_turned, xc_copied, qkv_made,
         qk_copied, v_copied, k_widened, scores_done, peaks_done, below_done, probs_done,
         probs_turned, probsT_copied, pv_done, rsum_done, o_done, o_turned, oT_copied, out_made,
         x_done) = (m.sem("a_" + n) for n in (
            "v_cleared", "stats_done", "mv_done", "eps_added", "rstd_done", "z_done", "xc_turned",
            "xc_copied", "qkv_made", "qk_copied", "v_copied", "k_widened",
            "scores_done", "peaks_done", "below_done", "probs_done", "probs_turned",
            "probsT_copied", "pv_done", "rsum_done", "o_done", "o_turned", "oT_copied",
            "out_made", "x_done"))
        block = ctx.enter_context(nc.Block())

        @block.sync
        def _(sp):
            sp.dma_start(xres[:, 0:FIRST, :], a["x"][0:FIRST].rearrange("t p d -> p t d")).then_inc(x_first_in, 16)
            for dst, src in ((wqT, "L0_xattn_wqT"), (wkT, "L0_xattn_wkT"), (wvT, "L0_xattn_wvT"),
                             (woT, "L0_xattn_woT")):
                sp.dma_start(dst[:], a[src]).then_inc(w_in, 16)
            sp.dma_start(gateT[:], a["L0_ffn_gate_wT"]).then_inc(w_in, 16)
            for dst, src in ((bq, "L0_xattn_bq"), (bk, "L0_xattn_bk"), (bv, "L0_xattn_bv")):
                sp.dma_start(dst[:], a[src].rearrange("(p o) -> p o", o=1)).then_inc(w_in, 16)
            sp.dma_start(bo[:], a["L0_xattn_bo"].rearrange("(o n) -> o n", o=1)).then_inc(w_in, 16)

            def body(s, k):
                if live(s, 0):
                    if since(s, UN):
                        sp.wait_ge(xc_turned, s - UN + 1)
                    sp.dma_start(context[:, k, :], a["ctx"][bass.ds(s, 1)].rearrange("o p d -> p (o d)")
                                 ).then_inc(context_in[k], 16)
                    if since(s, UN):
                        sp.wait_ge(w_low_done, s - UN + 1)
                    sp.dma_start(raw[:, k, :], a["split_w"][:, bass.ds(s * PART, PART)]).then_inc(raw_in[k], 16)

            slots(sp, body, 0)

        @block.vector
        def _(dve):
            dve.memset(v_wide[:], 0.0).then_inc(v_cleared, 1)
            dve.wait_ge(v_cleared, 1)
            for h in range(2):
                dve.memset(v_wide[h * S:(h + 1) * S, :, :, :, 2 * D0 + h:2 * D0 + h + 1],
                           1.0).then_inc(v_cleared, 1)

            dve.wait_ge(w_in, 9 * 16)
            dve.wait_ge(bv_turned, 1)
            dve.tensor_tensor(b_out[:], ps_out[0:1, 0:D], bo[:], ALU.add).then_inc(b_out_done, 1)

            def body(s, k):
                if live(s, 0):
                    b = k % 2
                    b0 = k % 2
                    if isinstance(s, int) and s == 0:
                        dve.wait_ge(x_first_in, 16)
                    if isinstance(s, int) and s == FIRST - 1:
                        dve.wait_ge(x_in, 16 * PARTS)
                    dve.bn_stats(stats[:, b0, :], xres[:, bass.ds(s, 1), :]).then_inc(stats_done, 1)
                if live(s, 7):
                    t, b2 = s - 7, (k - 7) % 2
                    if isinstance(s, int):
                        dve.wait_ge(x_done, t + 1)
                    dve.bn_stats(stats2[:, b2, :], xres[:, bass.ds(t, 1), :]).then_inc(stats2_done, 1)
                if live(s, 5):
                    t, b = s - 5, (k - 5) % 2
                    if live(s, 0):
                        dve.wait_ge(stats_done, s + 1)
                    if live(s, 7):
                        dve.wait_ge(stats2_done, s - 6)
                    dve.wait_ge(pv_done, t + 1)
                    dve.reciprocal(rsum[:, b, :].rearrange("p (c h) -> p c h", h=2),
                                   o_ps[:, :, 16:18]).then_inc(rsum_done, 1)
                    dve.wait_ge(rsum_done, t + 1)
                    if since(t, 2):
                        dve.wait_ge(o_turned, t - 1)
                    dve.tensor_tensor(
                        o[:, b, :].rearrange("p (c h d) -> p c h d", d=D0, h=2),
                        o_ps[:, :, 0:16].rearrange("p c (h d) -> p c h d", d=D0),
                        rsum[:, b, :].rearrange("p (c h o) -> p c h o", h=2, o=1).broadcast_to([P, 8, 2, D0]),
                        ALU.mult).then_inc(o_done, 1)
                if live(s, 10):
                    t = s - 10
                    dve.wait_ge(logits_made, t + 1)
                    dve.tensor_copy(logits[:, bass.ds(t, 1), :],
                                    ps_o[:, 8 * 18:8 * 18 + E].rearrange("p (o e) -> p o e", o=1)
                                    ).then_inc(logits_copied, 1)
                if live(s, 0):
                    if isinstance(s, int):
                        dve.wait_ge(stats_done, s + 1)
                    dve.bn_aggr(mean_var[:, b0, :], stats[:, b0, :]).then_inc(mv_done, 1)
                    dve.wait_ge(mv_done, s + 1)
                    dve.tensor_scalar(var_eps[:, b0, :], mean_var[:, b0, 1:2], EPS, None,
                                      ALU.add).then_inc(eps_added, 1)
                if live(s, 7):
                    t, b2, kt = s - 7, (k - 7) % 2, (k - 7) % UN
                    if isinstance(s, int):
                        dve.wait_ge(stats2_done, t + 1)
                    dve.bn_aggr(mean_var2[:, kt, :], stats2[:, b2, :]).then_inc(mv2_done, 1)
                    dve.wait_ge(mv2_done, t + 1)
                    dve.tensor_scalar(var_eps2[:, b2, :], mean_var2[:, kt, 1:2], EPS, None,
                                      ALU.add).then_inc(eps2_added, 1)
                if live(s, 6):
                    t = s - 6
                    dve.wait_ge(out_made, t + 1)
                    xt = xres[:, bass.ds(t, 1), :]
                    dve.scalar_tensor_tensor(xt, ps_out[:, P:2 * P].rearrange("p (o d) -> p o d", o=1),
                                             c["tanhs"][:, 0:1], xt,
                                             ALU.mult, ALU.add).then_inc(x_done, 1)
                if live(s, 3):
                    t, b = s - 3, (k - 3) % 2
                    for g in range(2):
                        dve.wait_ge(scores_done, 2 * t + g + 1)
                        sc = ps_s[g][:].rearrange("p (h n) -> p h n", n=S)
                        dve.tensor_reduce(peak[:, b, 8 * g:8 * g + 8], sc, AX.X, ALU.max).then_inc(peaks_done, 1)
                        dve.wait_ge(peaks_done, 2 * t + g + 1)
                        if since(t, 2) and g == 0:
                            dve.wait_ge(probs_done, t - 1)
                        dve.tensor_tensor(below[:, b, 8 * g:8 * g + 8, :], sc,
                                          peak[:, b, 8 * g:8 * g + 8].rearrange("p (h o) -> p h o", o=1)
                                          .broadcast_to([P, 8, S]), ALU.subtract).then_inc(below_done, 1)
                if live(s, 8):
                    t, b2, kt = s - 8, (k - 8) % 2, (k - 8) % UN
                    dve.wait_ge(rstd2_done, t + 1)
                    dve.wait_ge(x_done, s - 5 if not isinstance(s, int) else min(s - 5, NT))
                    if since(t, 2):
                        dve.wait_ge(z2_turned, t - 1)
                    dve.tensor_scalar(z2[:, b2, :], xres[:, bass.ds(t, 1), :].rearrange("p o d -> p (o d)"),
                                      mean_var2[:, kt, 0:1], rstd2[:, kt, :],
                                      ALU.subtract, ALU.mult).then_inc(z2_done, 1)
                if live(s, 3):
                    t, kt = s - 3, (k - 3) % UN
                    dve.wait_ge(w_high_done, t + 1)
                    dve.tensor_tensor(w_l[:, bass.ds(t * PART, PART)], raw[:, kt, :],
                                      w_h[:, bass.ds(t * PART, PART)], ALU.subtract).then_inc(w_low_done, 1)
                if live(s, 0):
                    b = k % 2
                    dve.wait_ge(rstd_done, s + 1)
                    if since(s, 2):
                        dve.wait_ge(xc_turned, s - 1)
                    dve.tensor_scalar(z[:, b, :], xres[:, bass.ds(s, 1), :].rearrange("p o d -> p (o d)"),
                                      mean_var[:, b, 0:1], rstd[:, b, :],
                                      ALU.subtract, ALU.mult).then_inc(z_done, 1)

            slots(dve, body, LAGS)

        @block.gpsimd
        def _(pool):
            def body(s, k):
                if live(s, 0):
                    b = k % 2
                    pool.wait_ge(eps_added, s + 1)
                    pool.tensor_tensor(rstd[:, b, :], var_eps[:, b, :], c["half_pow"][:, 0:1],
                                       ALU.pow).then_inc(rstd_done, 1)
                if live(s, 7):
                    b, kt = (k - 7) % 2, (k - 7) % UN
                    pool.wait_ge(eps2_added, s - 7 + 1)
                    pool.tensor_tensor(rstd2[:, kt, :], var_eps2[:, b, :], c["half_pow"][:, 0:1],
                                       ALU.pow).then_inc(rstd2_done, 1)
                if live(s, 2):
                    t, b = s - 2, (k - 2) % 2
                    pool.wait_ge(qk_copied, 2 * (t + 1))
                    if since(t, 2):
                        pool.wait_ge(scores_done, 2 * (t - 1))
                    pool.tensor_tensor(
                        k_wide[:, b], kT[:, b:b + 1, :].broadcast_to([P, H0, P]),
                        c["head_mask"][:].rearrange("p (h o) -> p h o", o=1).broadcast_to([P, H0, P]),
                        ALU.mult).then_inc(k_widened, 1)
                if live(s, 10):
                    t, kt = s - 10, (k - 10) % UN
                    pool.wait_ge(high_done, t + 1)
                    pool.tensor_tensor(zT_l[:, bass.ds(t, 1), :], zT[:, kt:kt + 1, :],
                                       zT_h[:, bass.ds(t, 1), :], ALU.subtract).then_inc(low_done, 1)

            slots(pool, body, LAGS)

        @block.scalar
        def _(act):
            for j in range(PARTS):
                n = (NT - FIRST) // PARTS
                part = slice(FIRST + j * n, FIRST + (j + 1) * n)
                act.dma_start(xres[:, part, :], a["x"][part].rearrange("t p d -> p t d")).then_inc(x_in, 16)
            act.wait_ge(v_cleared, 3)
            act.wait_ge(w_in, 9 * 16)

            def body(s, k):
                if live(s, 4):
                    t, b = s - 4, (k - 4) % 2
                    for g in range(2):
                        act.wait_ge(probs_turned, 2 * t + g + 1)
                        if since(t, 2) and g == 0:
                            act.wait_ge(pv_done, t - 1)
                        act.copy(probsT[:, b, 4 * g:4 * g + 4, :].rearrange("p c n -> p (c n)"),
                                 ps_pT[g][:]).then_inc(probsT_copied, 1)
                if live(s, 1):
                    t, b = s - 1, (k - 1) % 2
                    act.wait_ge(xc_turned, t + 1)
                    if since(t, 2):
                        act.wait_ge(qkv_made, t - 1)
                    act.copy(xT[:, b, :], ps_T[:, 0:P]).then_inc(xc_copied, 1)
                    act.copy(cT[:, b], ps_T[:, P:2 * P].rearrange("p (q o n) -> p q o n", q=2, o=1)
                             .broadcast_to([P, 2, 2, S])).then_inc(xc_copied, 1)
                if live(s, 9):
                    t, kt = s - 9, (k - 9) % UN
                    act.wait_ge(z2_turned, t + 1)
                    if since(t, UN):
                        act.wait_ge(low_done, t - UN + 1)
                        act.wait_ge(logits_made, t - UN + 1)
                    act.copy(zT[:, kt, :], ps_T[:, 2 * P:3 * P]).then_inc(z2_copied, 1)
                    act.wait_ge(z2_copied, t + 1)
                    act.copy(zT_h[:, bass.ds(t, 1), :], zT[:, kt:kt + 1, :]).then_inc(high_done, 1)
                if live(s, 5):
                    t, b = s - 5, (k - 5) % 2
                    act.wait_ge(o_turned, t + 1)
                    if since(t, 2):
                        act.wait_ge(out_made, t - 1)
                    act.copy(oT[:, b, :], ps_out[:, 0:P]).then_inc(oT_copied, 1)
                if live(s, 3):
                    t, b = s - 3, (k - 3) % 2
                    act.wait_ge(below_done, 2 * (t + 1))
                    if since(t, 2):
                        act.wait_ge(probs_turned, 2 * (t - 1))
                    act.activation(probs[:, b], below[:, b], ACT.Exp, scale=D0 ** -0.5).then_inc(probs_done, 1)
                if live(s, 2):
                    t, kt = s - 2, (k - 2) % UN
                    act.wait_ge(raw_in[kt], turn(t, kt))
                    act.copy(w_h[:, bass.ds(t * PART, PART)], raw[:, kt, :]).then_inc(w_high_done, 1)
                if live(s, 1):
                    t, b = s - 1, (k - 1) % 2
                    act.wait_ge(qkv_made, t + 1)
                    if since(t, 2):
                        act.wait_ge(k_widened, t - 1)
                    act.activation(kT[:, b, :], ps_qkv[:, P:2 * P], ACT.Identity,
                                   bias=bk[:]).then_inc(qk_copied, 1)
                    if since(t, 4):
                        act.wait_ge(pv_done, t - 3)
                    kt = (k - 1) % UN
                    act.activation(qT[:, kt, :], ps_qkv[:, 0:P], ACT.Identity,
                                   bias=bq[:]).then_inc(qk_copied, 1)
                    for h in range(2):
                        r = slice(h * S, (h + 1) * S)
                        act.copy(v_wide[r, kt, :, :, h * D0:(h + 1) * D0],
                                 ps_qkv[r, 2 * P:4 * P].rearrange("p (b c h d) -> p b c h d", b=2, c=8, h=2)
                                 [:, :, :, h, :]).then_inc(v_copied, 1)

            slots(act, body, LAGS)

        @block.tensor
        def _(pe):
            pe.wait_ge(w_in, 9 * 16)
            pe.matmul(ps_out[0:1, 0:D], bv[:], woT[:], start=True, stop=True).then_inc(bv_turned, 1)
            pe.wait_ge(b_out_done, 1)

            def body(s, k):
                if live(s, 10):
                    t, kt = s - 10, (k - 10) % UN
                    pe.wait_ge(z2_copied, t + 1)
                    pe.wait_ge(o_done, s - 5 if not isinstance(s, int) else min(s - 5, NT))
                    if since(t, 1):
                        pe.wait_ge(logits_copied, t)
                    pe.matmul(ps_o[:, 8 * 18:8 * 18 + E], zT[:, kt, :], gateT[:], start=True,
                              stop=True).then_inc(logits_made, 1)
                if live(s, 5):
                    t, b, kt = s - 5, (k - 5) % 2, (k - 5) % UN
                    pe.wait_ge(probsT_copied, 2 * (t + 1))
                    pe.wait_ge(v_copied, 2 * (t + 1))
                    if since(t, 1):
                        pe.wait_ge(o_done, t)
                    for q in range(2):
                        for j in range(8):
                            mm = pe.matmul(ps_o[q * S:(q + 1) * S, 18 * j:18 * j + 18],
                                           probsT[:, b, j, q * S:(q + 1) * S],
                                           v_wide[:, kt, q, j, :], start=True, stop=True)
                    mm.then_inc(pv_done, 1)
                if live(s, 4):
                    t, b = s - 4, (k - 4) % 2
                    pe.wait_ge(probs_done, t + 1)
                    for g in range(2):
                        if since(t, 1):
                            pe.wait_ge(probsT_copied, 2 * t - 1 + g)
                        for j in range(4):
                            h = 8 * g + 2 * j
                            mm = pe.transpose(ps_pT[g][:, j * P:(j + 1) * P],
                                              probs[:, b, h:h + 2, :].rearrange("p h n -> p (h n)"),
                                              c["ident"][:])
                        mm.then_inc(probs_turned, 1)
                if live(s, 9):
                    t, b = s - 9, (k - 9) % 2
                    pe.wait_ge(z2_done, t + 1)
                    pe.wait_ge(xc_copied, 2 * (s - 1) if not isinstance(s, int) else 2 * min(s - 1, NT))
                    if since(t, 1):
                        pe.wait_ge(z2_copied, t)
                    pe.transpose(ps_T[:, 2 * P:3 * P], z2[:, b, :], c["ident"][:]).then_inc(z2_turned, 1)
                if live(s, 1):
                    t, b, kt = s - 1, (k - 1) % 2, (k - 1) % UN
                    pe.wait_ge(z_done, t + 1)
                    if since(t, 1):
                        pe.wait_ge(xc_copied, 2 * t)
                    pe.transpose(ps_T[:, 0:P], z[:, b, :], c["ident"][:])
                    pe.wait_ge(context_in[kt], turn(t, kt))
                    pe.transpose(ps_T[:, P:2 * P], context[:, kt, :], c["ident"][:]).then_inc(xc_turned, 1)
                if live(s, 3):
                    t, b, kt = s - 3, (k - 3) % 2, (k - 3) % UN
                    pe.wait_ge(k_widened, t + 1)
                    pe.wait_ge(qk_copied, 2 * (t + 1))
                    for g in range(2):
                        if since(t, 1):
                            pe.wait_ge(below_done, 2 * t - 1 + g)
                        pe.matmul(ps_s[g][:], c["ident_b"][:],
                                  c["causal"][:].rearrange("p (o n) -> p o n", o=1).broadcast_to([P, 8, S]),
                                  start=True, stop=True, skip_group_check=True)
                        for q in range(2):
                            mm = pe.matmul(ps_s[g][q * S:(q + 1) * S, :], qT[:, kt, q * S:(q + 1) * S],
                                           k_wide[:, b, 8 * g:8 * g + 8, q * S:(q + 1) * S],
                                           start=False, stop=True, skip_group_check=True)
                        mm.then_inc(scores_done, 1)
                if live(s, 5):
                    t, b = s - 5, (k - 5) % 2
                    pe.wait_ge(o_done, t + 1)
                    if since(t, 1):
                        pe.wait_ge(x_done, t)
                    pe.transpose(ps_out[:, 0:P], o[:, b, :], c["ident"][:]).then_inc(o_turned, 1)
                if live(s, 1):
                    t, b = s - 1, (k - 1) % 2
                    pe.wait_ge(xc_copied, 2 * (t + 1))
                    if since(t, 1):
                        pe.wait_ge(qk_copied, 2 * t)
                        pe.wait_ge(v_copied, 2 * t)
                    pe.matmul(ps_qkv[:, P:2 * P], wkT[:], cT[:, b, :, 0, :], start=True, stop=True)
                    pe.matmul(ps_qkv[:, 0:P], wqT[:], xT[:, b, :], start=True, stop=True)
                    for q in range(2):
                        out = ps_qkv[:, (2 + q) * P:(3 + q) * P]
                        mm = pe.matmul(out, cT[:, b, q].rearrange("p o n -> p (o n)"), wvT[:], start=True, stop=True)
                    mm.then_inc(qkv_made, 1)
                if live(s, 5):
                    t, b = s - 5, (k - 5) % 2
                    pe.wait_ge(oT_copied, t + 1)
                    pe.matmul(ps_out[:, P:2 * P], oT[:, b, :], woT[:], start=True, stop=False)
                    pe.matmul(ps_out[:, P:2 * P], c["ones_row"][:], b_out[:], start=False, stop=True).then_inc(out_made, 1)

            slots(pe, body, LAGS)


def at(j, k, lag, un):
    return j + (k - lag) // un, (k - lag) % un


def turns(eng, body, lags, count, un):
    first = -(-(lags + 2) // un)
    for j in range(first):
        for k in range(un):
            body(j, k)
    with eng.Fori(first, count // un) as j:
        for k in range(un):
            body(j, k)
    for s in range(count, count + lags):
        body(s // un, s % un)


def perceiver(nc, c, xres, a, w_h, w_l):
    UNG, G, HALF = 8, 4 * NT, 512
    LAGS = 13
    with ExitStack() as ctx:
        m = Mem(nc, ctx, "perc_")
        w_out = m.sb("w_out", [P, H1 // 2, D])
        gain = m.sb("gain", [P, 2])
        shift = m.sb("shift", [P, 2])
        norm_gains = m.sb("norm_gains", [P, 2])
        qk_gain = m.sb("qk_gain", [P, 1])
        b_out = m.sb("b_out", [1, D])
        ones_b = m.sb("ones_b", [1, P], BF16)
        context = m.sb("context2", [P, 2, D])
        mask_in = m.sb("mask_in", [1, 2, 2, S], U8)
        mask_row = m.sb("mask_row", [1, 2, 2, P], BF16)
        stats = m.sb("stats2", [P, 2, 2, 6])
        mean_var = m.sb("mean_var2", [P, 2, 2, 2])
        var_eps = m.sb("var_eps2", [P, 2, 2])
        rstd = m.sb("rstd2", [P, 2, 2])
        z = m.sb("z2", [P, 2, 2, D])
        zT = m.sb("zT", [P, 2, 2, P])
        keys_h, keys_l = (m.sb(n, [P, 2, 2, P], BF16) for n in ("keys_h", "keys_l"))
        lat_h, lat_l = (m.sb(n, [P, 2, P], BF16) for n in ("lat_h", "lat_l"))
        squares = m.sb("squares", [P, 3, HALF])
        square_sums = m.sb("square_sums", [P, 3, 8])
        rnorm = m.sb("rnorm", [P, 3, 8])
        qk_n = m.sb("qk_n", [P, 3, HALF])
        kT = m.sb("kT2", [P, 2, 4, P])
        q_diag = m.sb("q_diag", [P, 2, 4, 2, P])
        v = m.sb("v", [P, 4, HALF])
        neg_peak = m.sb("neg_peak", [P, 2, 4])
        sums = m.sb("sums", [P, 2, 4])
        rsum = m.sb("rsum2", [P, 2, 4])
        probs = m.sb("probs2", [P, 2, 4, P])
        probs_n = m.sb("probs_n", [P, 2, 4, P])
        probsT = m.sb("probsT2", [P, 2, 4, P])
        oT = m.sb("oT2", [P, 2, H1 // 2, 2, S])

        ps_kq = [m.ps(f"ps_kq{i}") for i in range(3)]
        ps_s = [m.ps("ps_s0"), m.ps("ps_s1")]
        ps_vp, ps_o = m.ps("ps_vp"), m.ps("ps_o")
        ps_t = m.ps("ps_t")

        w_in = m.sem("c_w_in")
        tile_in = [m.sem(f"c_tile_in{k}") for k in range(2)]
        names = ("ready", "stats_done", "mv_done", "eps_added", "rstd_done", "z_done", "z_turned", "zT_done",
                 "keys_h_done", "keys_l_done", "lat_done", "mask_done", "kq_made", "squared", "reduced",
                 "rnorm_done", "kq_normed", "v_made", "v_copied", "k_turned", "q_turned",
                 "kT_copied", "q_copied", "scores_done", "peaks_done", "probs_done", "rsum_done",
                 "probs_normed", "probs_turned", "probsT_copied", "o_made", "o_copied", "y_made", "x_done")
        sem = {n: m.sem("c_" + n) for n in names}
        (ready, stats_done, mv_done, eps_added, rstd_done, z_done, z_turned, zT_done,
         keys_h_done, keys_l_done, lat_done, mask_done, kq_made, squared, reduced,
         rnorm_done, kq_normed, v_made, v_copied, k_turned, q_turned,
         kT_copied, q_copied, scores_done, peaks_done, probs_done, rsum_done,
         probs_normed, probs_turned, probsT_copied, o_made, o_copied, y_made, x_done) = (sem[n] for n in names)
        NW = 10
        block = ctx.enter_context(nc.Block())

        def group(j, k, lag):
            j, k = at(j, k, lag, UNG)
            g = j * UNG + k
            return not isinstance(j, int) or 0 <= g < G, j, k, g

        def past(x, least):
            return not isinstance(x, int) or x >= least

        def use(j, k, keys):
            return 12 * j + 3 * (k // 2) + (0 if not keys else 1 + k % 2)

        @block.sync
        def _(sp):
            sp.dma_start(w_out[:], a["L1_xattn_Wout"].rearrange("(c p) n -> p c n", p=P)).then_inc(w_in, 16)
            for col, (g_, b_) in enumerate((("ln_x_g", "ln_x_b"), ("ln_l_g", "ln_l_b"))):
                sp.dma_start(gain[:, col:col + 1], a["L1_xattn_" + g_].rearrange("(p o) -> p o", o=1)).then_inc(w_in, 16)
                sp.dma_start(shift[:, col:col + 1], a["L1_xattn_" + b_].rearrange("(p o) -> p o", o=1)).then_inc(w_in, 16)
            for h in range(2):
                for col, n in enumerate(("qn_g", "kn_g")):
                    sp.dma_start(norm_gains[h * D1:(h + 1) * D1, col:col + 1],
                                 a["L1_xattn_" + n].rearrange("(p o) -> p o", o=1)).then_inc(w_in, 16)
            sp.dma_start(b_out[:], a["L1_xattn_bout"].rearrange("(o n) -> o n", o=1)).then_inc(w_in, 16)

            def body(t, b):
                if past(t, 2):
                    sp.wait_ge(z_done, 2 * (t - 1))
                    sp.wait_ge(mask_done, t - 1)
                sp.dma_start(context[:, b, :], a["ctx"][bass.ds(t, 1)].rearrange("o p d -> p (o d)")
                             ).then_inc(tile_in[b], 16)
                sp.dma_start(mask_in[:, b], a["mask"][bass.ds(t * 2, 2)].rearrange("(o b) n -> o b n", o=1)
                             ).then_inc(tile_in[b], 16)

            for t in range(2):
                body(t, t)
            with sp.Fori(1, NT // 2) as j:
                for b in range(2):
                    body(j * 2 + b, b)

        @block.gpsimd
        def _(pool):
            pool.memset(mask_row[:], 0.0).then_inc(ready, 1)
            pool.memset(ones_b[:], 1.0).then_inc(ready, 1)
            pool.wait_ge(ready, 4)

            def body(j, k):
                ok, jj, kk, g = group(j, k, 3)
                if ok:
                    for keys in ([False, True] if kk % 2 == 0 else [True]):
                        n = use(jj, kk, keys)
                        pool.wait_ge(reduced, n + 1)
                        b = use(0, kk, keys) % 3
                        pool.tensor_tensor(rnorm[:, b], square_sums[:, b], c["half_pow"][:, 0:8],
                                           ALU.pow).then_inc(rnorm_done, 1)
                ok, jj, kk, g = group(j, k, 0)
                if ok and kk % 4 == 0:
                    t, b = 2 * jj + kk // 4, kk // 4
                    pool.wait_ge(eps_added, 2 * (t + 1))
                    pool.tensor_tensor(rstd[:, b, :], var_eps[:, b, :], c["half_pow"][:, 0:2],
                                       ALU.pow).then_inc(rstd_done, 1)
                ok, jj, kk, g = group(j, k, 2)
                if ok and kk % 4 == 0:
                    t, b = 2 * jj + kk // 4, kk // 4
                    pool.wait_ge(keys_h_done, t + 1)
                    pool.tensor_tensor(keys_l[:, b].rearrange("p q (s n) -> p s q n", s=2),
                                       zT[:, b].rearrange("p s (q n) -> p s q n", q=2),
                                       keys_h[:, b].rearrange("p q (s n) -> p s q n", s=2),
                                       ALU.subtract).then_inc(keys_l_done, 1)
                    pool.tensor_copy(lat_h[:, b].rearrange("p (q n) -> p q n", q=2),
                                     keys_h[:, b, :, S:P]).then_inc(lat_done, 1)
                    pool.wait_ge(lat_done, 2 * t + 1)
                    pool.tensor_tensor(lat_l[:, b], zT[:, b, 1], lat_h[:, b], ALU.subtract).then_inc(lat_done, 1)

            turns(pool, body, LAGS, G, UNG)

        @block.scalar
        def _(act):
            act.wait_ge(w_in, 16 * NW)
            act.wait_ge(ready, 4)

            def copy_keys(kk, g):
                act.wait_ge(k_turned, g + 1)
                if past(g, 2):
                    act.wait_ge(scores_done, g - 1)
                act.copy(kT[:, kk % 2].rearrange("p u n -> p (u n)"), ps_t[:]).then_inc(kT_copied, 1)

            def body(j, k):
                ok, jj, kk, g = group(j, k, 5)
                if ok and kk % 2 == 0:
                    pair, hb = 4 * jj + kk // 2, (kk // 2) % 2
                    act.wait_ge(q_turned, pair + 1)
                    if past(pair, 2):
                        act.wait_ge(scores_done, 2 * (pair - 1))
                    for h in range(2):
                        r = slice(h * S, (h + 1) * S)
                        act.activation(q_diag[r, hb, :, :, h * S:(h + 1) * S],
                                       ps_t[r, :].rearrange("p (u q n) -> p u q n", u=4, q=2),
                                       ACT.Identity, scale=qk_gain[r, :]).then_inc(q_copied, 1)
                if ok and kk % 2 == 1:
                    copy_keys(kk, g)
                ok, jj, kk, g = group(j, k, 7)
                if ok:
                    act.wait_ge(v_made, g + 1)
                    if past(g, 4):
                        act.wait_ge(o_made, g - 3)
                    act.copy(v[:, kk % 4], ps_vp[:]).then_inc(v_copied, 1)
                ok, jj, kk, g = group(j, k, 7)
                if ok:
                    b = kk % 2
                    act.wait_ge(peaks_done, g + 1)
                    if past(g, 2):
                        act.wait_ge(probs_normed, 4 * (g - 1))
                    for u in range(4):
                        act.activation(probs[:, b, u], ps_s[b][:, u * P:(u + 1) * P], ACT.Exp,
                                       bias=neg_peak[:, b, u:u + 1],
                                       accum_out=sums[:, b, u:u + 1]).then_inc(probs_done, 1)
                ok, jj, kk, g = group(j, k, 5)
                if ok and kk % 2 == 0:
                    copy_keys(kk, g)
                ok, jj, kk, g = group(j, k, 3)
                if ok:
                    for keys in ([False, True] if kk % 2 == 0 else [True]):
                        n, b = use(jj, kk, keys), use(0, kk, keys) % 3
                        act.wait_ge(kq_made, n + 1)
                        if past(n, 3):
                            act.wait_ge(reduced, n - 2)
                        act.square(squares[:, b], ps_kq[b][:]).then_inc(squared, 1)
                ok, jj, kk, g = group(j, k, 8)
                if ok:
                    b = kk % 2
                    act.wait_ge(probs_turned, g + 1)
                    if past(g, 2):
                        act.wait_ge(o_made, g - 1)
                    act.copy(probsT[:, b].rearrange("p u n -> p (u n)"), ps_vp[:]).then_inc(probsT_copied, 1)
                ok, jj, kk, g = group(j, k, 2)
                if ok and kk % 4 == 0:
                    t, b = 2 * jj + kk // 4, kk // 4
                    act.wait_ge(z_turned, t + 1)
                    if past(t, 2):
                        act.wait_ge(lat_done, 2 * (t - 1))
                    for src in range(2):
                        act.activation(zT[:, b, src], ps_t[:, src * P:(src + 1) * P], ACT.Identity,
                                       bias=shift[:, src:src + 1], scale=gain[:, src:src + 1]).then_inc(zT_done, 1)
                    act.wait_ge(zT_done, 2 * (t + 1))
                    if past(t, 2):
                        act.wait_ge(v_made, 4 * (t - 1))
                    act.copy(keys_h[:, b].rearrange("p q (s n) -> p s q n", s=2),
                             zT[:, b].rearrange("p s (q n) -> p s q n", q=2)).then_inc(keys_h_done, 1)

            turns(act, body, LAGS, G, UNG)

        @block.vector
        def _(dve):
            dve.memset(q_diag[:], 0.0).then_inc(ready, 1)
            dve.wait_ge(w_in, 16 * NW)
            dve.scalar_tensor_tensor(qk_gain[:], norm_gains[:, 0:1], D1 ** -0.5 * D1, norm_gains[:, 1:2],
                                     ALU.mult, ALU.mult).then_inc(ready, 1)

            def body(j, k):
                ok, jj, kk, g = group(j, k, 3)
                if ok and kk % 4 == 0:
                    t, b = 2 * jj + kk // 4, kk // 4
                    dve.wait_ge(tile_in[b], 32 * (jj + 1))
                    if past(t, 2):
                        dve.wait_ge(scores_done, 4 * (t - 1))
                    dve.tensor_scalar(mask_row[:, b, :, 0:S], mask_in[:, b], -FAR, FAR,
                                       ALU.mult, ALU.add).then_inc(mask_done, 1)
                ok, jj, kk, g = group(j, k, 7)
                if ok:
                    b = kk % 2
                    dve.wait_ge(scores_done, g + 1)
                    dve.tensor_reduce(neg_peak[:, b], ps_s[b][:].rearrange("p (u n) -> p u n", u=4), AX.X,
                                      ALU.max, negate=True).then_inc(peaks_done, 1)
                ok, jj, kk, g = group(j, k, 8)
                if ok:
                    b = kk % 2
                    dve.wait_ge(probs_done, 4 * (g + 1))
                    dve.reciprocal(rsum[:, b], sums[:, b]).then_inc(rsum_done, 1)
                    dve.wait_ge(rsum_done, g + 1)
                    if past(g, 2):
                        dve.wait_ge(probs_turned, g - 1)
                    for u in range(4):
                        dve.tensor_scalar(probs_n[:, b, u], probs[:, b, u], rsum[:, b, u:u + 1], None,
                                          ALU.mult).then_inc(probs_normed, 1)
                ok, jj, kk, g = group(j, k, 1)
                if ok and kk % 4 == 0:
                    t, b = 2 * jj + kk // 4, kk // 4
                    xt = xres[:, bass.ds(t, 1), :].rearrange("p o d -> p (o d)")
                    dve.wait_ge(rstd_done, t + 1)
                    if past(t, 2):
                        dve.wait_ge(z_turned, t - 1)
                    for src, rows_ in enumerate((context[:, b, :], xt)):
                        dve.tensor_scalar(z[:, b, src], rows_, mean_var[:, b, src, 0:1], rstd[:, b, src:src + 1],
                                          ALU.subtract, ALU.mult).then_inc(z_done, 1)
                ok, jj, kk, g = group(j, k, 0)
                if ok and kk % 4 == 0:
                    t, b = 2 * jj + kk // 4, kk // 4
                    xt = xres[:, bass.ds(t, 1), :].rearrange("p o d -> p (o d)")
                    dve.wait_ge(tile_in[b], 32 * (jj + 1))
                    dve.bn_stats(stats[:, b, 0], context[:, b, :]).then_inc(stats_done, 1)
                    dve.bn_stats(stats[:, b, 1], xt).then_inc(stats_done, 1)
                stats_of = (2 * jj + kk // 4) if ok and kk % 4 == 0 else None
                ok, jj, kk, g = group(j, k, 9)
                if ok:
                    tb, half, q = kk // 4, (kk // 2) % 2, kk % 2
                    if stats_of is not None:
                        dve.wait_ge(stats_done, 2 * (stats_of + 1))
                    dve.wait_ge(o_made, g + 1)
                    if kk % 4 == 0 and past(g, 8):
                        dve.wait_ge(y_made, 2 * jj + kk // 4 - 1)
                    for h in range(2):
                        r = slice(h * S, (h + 1) * S)
                        dve.tensor_copy(oT[r, tb, 4 * half:4 * half + 4, q, :],
                                        ps_o[r, :].rearrange("p (u h n) -> p u h n", u=4, h=2)[:, :, h, :]
                                        ).then_inc(o_copied, 1)
                ok, jj, kk, g = group(j, k, 4)
                for keys in [] if not ok else [False, True] if kk % 2 == 0 else [True]:
                    n, b = use(jj, kk, keys), use(0, kk, keys) % 3
                    dve.wait_ge(rnorm_done, n + 1)
                    if not keys and past(jj * 4 + kk // 2, 1):
                        dve.wait_ge(q_turned, jj * 4 + kk // 2)
                    if keys and past(g, 2):
                        dve.wait_ge(k_turned, g - 1)
                    dve.scalar_tensor_tensor(qk_n[:, b].rearrange("p (h d) -> p h d", d=D1),
                                             rnorm[:, b].rearrange("p (h o) -> p h o", o=1)
                                             .broadcast_to([P, 8, D1]), 1e8 / 8,
                                             ps_kq[b][:].rearrange("p (h d) -> p h d", d=D1),
                                             ALU.min, ALU.mult).then_inc(kq_normed, 1)
                ok, jj, kk, g = group(j, k, 13)
                if ok and kk % 4 == 3:
                    t = 2 * jj + kk // 4
                    dve.wait_ge(y_made, t + 1)
                    xt = xres[:, bass.ds(t, 1), :]
                    dve.scalar_tensor_tensor(xt, ps_t[:, 0:P].rearrange("p (o d) -> p o d", o=1),
                                             c["tanhs"][:, 1:2], xt, ALU.mult, ALU.add).then_inc(x_done, 1)
                ok, jj, kk, g = group(j, k, 3)
                for keys in [] if not ok else [False, True] if kk % 2 == 0 else [True]:
                    n, b = use(jj, kk, keys), use(0, kk, keys) % 3
                    dve.wait_ge(squared, n + 1)
                    dve.reduce_sum(square_sums[:, b], squares[:, b].rearrange("p (h d) -> p h d", d=D1),
                                   AX.X).then_inc(reduced, 1)
                ok, jj, kk, g = group(j, k, 0)
                if ok and kk % 4 == 0:
                    t, b = 2 * jj + kk // 4, kk // 4
                    if isinstance(t, int):
                        dve.wait_ge(stats_done, 2 * (t + 1))
                    for src in range(2):
                        dve.bn_aggr(mean_var[:, b, src], stats[:, b, src]).then_inc(mv_done, 1)
                    dve.wait_ge(mv_done, 2 * (t + 1))
                    dve.tensor_scalar(var_eps[:, b, 0:1], mean_var[:, b, 0, 1:2], EPS, None,
                                      ALU.add).then_inc(eps_added, 1)
                    dve.tensor_scalar(var_eps[:, b, 1:2], mean_var[:, b, 1, 1:2], 1.0 + EPS, EPS * EPS,
                                      ALU.mult, ALU.add).then_inc(eps_added, 1)

            turns(dve, body, LAGS, G, UNG)

        @block.tensor
        def _(pe):
            pe.wait_ge(w_in, 16 * NW)
            pe.wait_ge(ready, 4)

            def three(out, sh, sl, mh, ml):
                pe.matmul(out, sh, mh, start=True, stop=False)
                pe.matmul(out, sh, ml, start=False, stop=False)
                return pe.matmul(out, sl, mh, start=False, stop=True)

            def turn_keys(jj, kk, g):
                if kk % 2 == 0:
                    pe.wait_ge(q_copied, 2 * (4 * jj + kk // 2 + 1))
                else:
                    pe.wait_ge(kT_copied, g)
                pe.wait_ge(kq_normed, use(jj, kk, True) + 1)
                for u in range(4):
                    mm = pe.transpose(ps_t[:, u * P:(u + 1) * P],
                                      qk_n[:, 1 + kk % 2, u * P:(u + 1) * P], c["ident"][:])
                mm.then_inc(k_turned, 1)

            def body(j, k):
                ok, jj, kk, g = group(j, k, 5)
                if ok and kk % 2 == 0:
                    pe.wait_ge(kq_normed, use(jj, kk, False) + 1)
                    t = 2 * jj + kk // 4
                    if kk % 4 == 0 and past(t, 3):
                        pe.wait_ge(x_done, t - 2)
                    elif kk % 4 == 2 and not (isinstance(t, int) and t + 1 >= NT):
                        pe.wait_ge(zT_done, 2 * (t + 2))
                    elif past(g, 1):
                        pe.wait_ge(kT_copied, g)
                    for u in range(4):
                        mm = pe.transpose(ps_t[:, u * P:(u + 1) * P], qk_n[:, 0, u * P:(u + 1) * P],
                                          c["ident"][:])
                    mm.then_inc(q_turned, 1)
                if ok and kk % 2 == 1:
                    turn_keys(jj, kk, g)
                ok, jj, kk, g = group(j, k, 7)
                if ok:
                    tb, half, q = kk // 4, (kk // 2) % 2, kk % 2
                    cols = slice(W_KV + INNER + half * HALF, W_KV + INNER + (half + 1) * HALF)
                    if past(g, 2):
                        pe.wait_ge(probsT_copied, g - 1)
                    elif past(g, 1):
                        pe.wait_ge(v_copied, g)
                    three(ps_vp[:], keys_h[:, tb, q], keys_l[:, tb, q], w_h[:, cols],
                          w_l[:, cols]).then_inc(v_made, 1)
                ok, jj, kk, g = group(j, k, 9)
                if ok:
                    b = kk % 2
                    pe.wait_ge(probsT_copied, g + 1)
                    if past(g, 1):
                        pe.wait_ge(o_copied, 2 * g)
                    for u in range(4):
                        mm = pe.matmul(ps_o[:, u * P:(u + 1) * P], v[:, kk % 4, u * P:(u + 1) * P],
                                       probsT[:, b, u], start=True, stop=True)
                    mm.then_inc(o_made, 1)
                ok, jj, kk, g = group(j, k, 5)
                if ok and kk % 2 == 0:
                    turn_keys(jj, kk, g)
                ok, jj, kk, g = group(j, k, 2)
                if ok and kk % 4 == 0:
                    t, b = 2 * jj + kk // 4, kk // 4
                    pe.wait_ge(z_done, 2 * (t + 1))
                    if past(t, 1):
                        pe.wait_ge(kT_copied, 4 * t - 2)
                    pe.transpose(ps_t[:, 0:P], z[:, b, 0], c["ident"][:])
                    pe.transpose(ps_t[:, P:2 * P], z[:, b, 1], c["ident"][:]).then_inc(z_turned, 1)
                ok, jj, kk, g = group(j, k, 13)
                if ok and kk % 4 == 3:
                    t, tb = 2 * jj + kk // 4, kk // 4
                    pe.wait_ge(o_copied, 2 * (g + 1))
                    if isinstance(t, int) and t + 3 > NT:
                        pe.wait_ge(x_done, t)
                    else:
                        pe.wait_ge(kT_copied, 4 * (t + 3))
                    for u in range(H1 // 2):
                        pe.matmul(ps_t[:, 0:P], oT[:, tb, u].rearrange("p q n -> p (q n)"), w_out[:, u, :],
                                  start=(u == 0), stop=False)
                    pe.matmul(ps_t[:, 0:P], c["ones_row"][:], b_out[:], start=False, stop=True).then_inc(y_made, 1)
                ok, jj, kk, g = group(j, k, 8)
                if ok:
                    b = kk % 2
                    pe.wait_ge(probs_normed, 4 * (g + 1))
                    pe.wait_ge(v_copied, g + 2 if not isinstance(g, int) else min(g + 2, G))
                    for u in range(4):
                        mm = pe.transpose(ps_vp[:, u * P:(u + 1) * P], probs_n[:, b, u], c["ident"][:])
                    mm.then_inc(probs_turned, 1)
                ok, jj, kk, g = group(j, k, 3)
                if ok:
                    t, tb, half, q = 2 * jj + kk // 4, kk // 4, (kk // 2) % 2, kk % 2
                    k_cols = slice(W_KV + half * HALF, W_KV + (half + 1) * HALF)
                    q_cols = slice(W_Q + half * HALF, W_Q + (half + 1) * HALF)
                    if kk % 4 == 0:
                        pe.wait_ge(keys_l_done, t + 1)
                        pe.wait_ge(lat_done, 2 * (t + 1))
                    for keys in ([False, True] if kk % 2 == 0 else [True]):
                        n, b = use(jj, kk, keys), use(0, kk, keys) % 3
                        if past(n, 3):
                            pe.wait_ge(kq_normed, n - 2)
                        if keys:
                            mm = three(ps_kq[b][:], keys_h[:, tb, q], keys_l[:, tb, q], w_h[:, k_cols], w_l[:, k_cols])
                        else:
                            mm = three(ps_kq[b][:], lat_h[:, tb], lat_l[:, tb], w_h[:, q_cols], w_l[:, q_cols])
                        mm.then_inc(kq_made, 1)
                ok, jj, kk, g = group(j, k, 6)
                if ok:
                    b, tb, hb, q = kk % 2, kk // 4, (kk // 2) % 2, kk % 2
                    if kk % 4 == 0:
                        pe.wait_ge(mask_done, 2 * jj + kk // 4 + 1)
                    if kk % 2 == 0:
                        pe.wait_ge(q_copied, 2 * (4 * jj + kk // 2 + 1))
                    pe.wait_ge(kT_copied, g + 1)
                    if past(g, 2):
                        pe.wait_ge(probs_done, 4 * (g - 1))
                    pe.matmul(ps_s[b][:], ones_b[:], mask_row[:, tb, q:q + 1, :].broadcast_to([1, 4, P]),
                              start=True, stop=True, skip_group_check=True)
                    for u in range(4):
                        mm = pe.matmul(ps_s[b][:, u * P:(u + 1) * P], q_diag[:, hb, u, q], kT[:, b, u],
                                       start=False, stop=True, skip_group_check=True)
                    mm.then_inc(scores_done, 1)

            turns(pe, body, LAGS, G, UNG)


def route(nc, c, logits, weight):
    with ExitStack() as ctx:
        m = Mem(nc, ctx, "route_")
        first_key = m.sb("first_key", [P, E])
        keyed, hot1, hot2, rest = (m.sb(n, [P, NT, E]) for n in ("keyed", "hot1", "hot2", "rest"))
        top1, top2, best, gap, odds, p1, p2 = (
            m.sb(n, [P, NT]) for n in ("top1", "top2", "best", "gap", "odds", "p1", "p2"))
        keys_made, chain, odds_done = (m.sem("r_" + n) for n in ("keys_made", "chain", "odds_done"))
        block = ctx.enter_context(nc.Block())

        @block.gpsimd
        def _(pool):
            for e in range(E):
                pool.memset(first_key[:, e:e + 1], float(E - e)).then_inc(keys_made, 1)

        @block.scalar
        def _(act):
            act.wait_ge(chain, 12)
            act.activation(odds[:], gap[:], ACT.Exp).then_inc(odds_done, 1)

        @block.vector
        def _(dve):
            dve.wait_ge(keys_made, E)

            def wide(v):
                return v.rearrange("p (t o) -> p t o", o=1).broadcast_to([P, NT, E])

            done = [0]

            def then(ins):
                done[0] += 1
                ins.then_inc(chain, 1)
                dve.wait_ge(chain, done[0])

            keys = first_key[:].rearrange("p (o e) -> p o e", o=1).broadcast_to([P, NT, E])
            for src, top, hot in ((logits, top1, hot1), (rest, top2, hot2)):
                then(dve.tensor_reduce(top[:], src[:], AX.X, ALU.max))
                then(dve.tensor_tensor(keyed[:], src[:], wide(top[:]), ALU.is_equal))
                then(dve.tensor_tensor(keyed[:], keyed[:], keys, ALU.mult))
                then(dve.tensor_reduce(best[:], keyed[:], AX.X, ALU.max))
                then(dve.tensor_tensor(hot[:], keyed[:], wide(best[:]), ALU.is_equal))
                if src is logits:
                    then(dve.scalar_tensor_tensor(rest[:].rearrange("p t e -> p (t e)"),
                                                  hot1[:].rearrange("p t e -> p (t e)"), -3e38,
                                                  logits[:].rearrange("p t e -> p (t e)"), ALU.mult, ALU.add))
            then(dve.tensor_tensor(gap[:], top2[:], top1[:], ALU.subtract))
            dve.wait_ge(odds_done, 1)
            then(dve.tensor_scalar(p2[:], odds[:], 1.0, None, ALU.add))
            then(dve.reciprocal(p1[:], p2[:]))
            then(dve.tensor_scalar(p1[:], p1[:], c["tanhs"][:, 2:3], None, ALU.mult))
            then(dve.tensor_tensor(p2[:], p1[:], odds[:], ALU.mult))
            then(dve.tensor_tensor(hot1[:], hot1[:], wide(p1[:]), ALU.mult))
            then(dve.tensor_tensor(hot2[:], hot2[:], wide(p2[:]), ALU.mult))
            then(dve.tensor_tensor(weight[:], hot1[:], hot2[:], ALU.add))


def experts(nc, c, xres, zT_h, zT_l, logits, w_h, w_l):
    UNIT, T4, LAGS = E, 4, 1
    CH = I // P
    with ExitStack() as ctx:
        m = Mem(nc, ctx, "moe_")
        weight = m.sb("weight", [P, NT, E])
        route(nc, c, logits, weight)
        gate = m.sb("gate", [P, 2, 512])
        hid = m.sb("hid", [P, 2, 512])
        hid_h, hid_l = (m.sb(n, [P, 2, CH, 512], BF16) for n in ("hid_h", "hid_l"))
        ps_g, ps_u, ps_d = ([m.ps(f"ps_{n}{i}") for i in range(2)] for n in "gud")
        names = ("gate_made", "up_made", "silu_done", "hid_done", "high_done", "low_done", "down_made", "x_done")
        gate_made, up_made, silu_done, hid_done, high_done, low_done, down_made, x_done = (
            m.sem("b_" + n) for n in names)
        block = ctx.enter_context(nc.Block())
        NG = NT // T4
        N = NG * E

        def unit(j, e, lag):
            j, e = at(j, e, lag, E)
            n = j * E + e
            return not isinstance(n, int) or 0 <= n < N, j, e, n

        def past(x, least):
            return not isinstance(x, int) or x >= least

        @block.tensor
        def _(pe):
            def body(j, k):
                for i in range(CH):
                    ok, g, e, n = unit(j, k, 0)
                    if ok:
                        b = i % 2
                        zh = zT_h[:, bass.ds(g * T4, T4), :]
                        zl = zT_l[:, bass.ds(g * T4, T4), :]
                        for first, out, made, used in ((W_GATE, ps_g[b], gate_made, silu_done),
                                                       (W_UP, ps_u[b], up_made, hid_done)):
                            cols = slice(first + e * I + i * P, first + e * I + (i + 1) * P)
                            if past(CH * n + i, 2):
                                pe.wait_ge(used, CH * n + i - 1)
                            pe.matmul(out[:], w_h[:, cols], zh, start=True, stop=False)
                            pe.matmul(out[:], w_h[:, cols], zl, start=False, stop=False)
                            pe.matmul(out[:], w_l[:, cols], zh, start=False, stop=True).then_inc(made, 1)
                    ok, g, e, n = unit(j, k, 1)
                    if ok:
                        b = e % 2
                        if i == 0 and past(n, 2):
                            pe.wait_ge(x_done, T4 * (n - 1))
                        pe.wait_ge(low_done, CH * n + i + 1)
                        cols = slice(W_DOWN + e * I + i * P, W_DOWN + e * I + (i + 1) * P)
                        for t in range(T4):
                            rows_ = slice(t * P, (t + 1) * P)
                            for p, (h, w) in enumerate(((hid_h, w_h), (hid_h, w_l), (hid_l, w_h))):
                                mm = pe.matmul(ps_d[b][:, rows_], h[:, b, i, rows_], w[:, cols],
                                               start=(i == 0 and t == 0 and p == 0), stop=(i == CH - 1 and p == 2),
                                               skip_group_check=True)
                        if i == CH - 1:
                            mm.then_inc(down_made, 1)

            turns(pe, body, LAGS, N, E)

        @block.scalar
        def _(act):
            def body(j, k):
                ok, g, e, n = unit(j, k, 0)
                if not ok:
                    return
                for i in range(CH):
                    b, q = i % 2, CH * n + i
                    act.wait_ge(gate_made, q + 1)
                    if past(q, 2):
                        act.wait_ge(hid_done, q - 1)
                    act.activation(gate[:, b], ps_g[b][:], ACT.Silu).then_inc(silu_done, 1)
                    if i >= 1:
                        high(act, n, e, i - 1)
                high(act, n, e, CH - 1)

            def high(act, n, e, i):
                q = CH * n + i
                act.wait_ge(hid_done, q + 1)
                if i == 0 and past(n, 2):
                    act.wait_ge(down_made, n - 1)
                act.copy(hid_h[:, e % 2, i], hid[:, i % 2]).then_inc(high_done, 1)

            turns(act, body, LAGS, N, E)

        @block.vector
        def _(dve):
            def low(n, e, i):
                q = CH * n + i
                dve.wait_ge(high_done, q + 1)
                dve.tensor_tensor(hid_l[:, e % 2, i], hid[:, i % 2], hid_h[:, e % 2, i],
                                  ALU.subtract).then_inc(low_done, 1)

            def body(j, k):
                ok, g, e, n = unit(j, k, 0)
                if ok:
                    for i in range(CH):
                        b, q = i % 2, CH * n + i
                        dve.wait_ge(silu_done, q + 1)
                        dve.wait_ge(up_made, q + 1)
                        if i == 0 and past(n, 2):
                            dve.wait_ge(down_made, n - 1)
                        if past(q, 2):
                            dve.wait_ge(low_done, q - 1)
                        dve.tensor_tensor(hid[:, b], gate[:, b], ps_u[b][:], ALU.mult).then_inc(hid_done, 1)
                        if i >= 1:
                            low(n, e, i - 1)
                    low(n, e, CH - 1)
                ok, g, e, n = unit(j, k, 1)
                if ok:
                    dve.wait_ge(down_made, n + 1)
                    for t in range(T4):
                        if past(n, 1):
                            dve.wait_ge(x_done, T4 * (n - 1) + t + 1)
                        xt = xres[:, bass.ds(g * T4 + t, 1), :].rearrange("p o d -> p (o d)")
                        wt = weight[:, bass.ds(g * T4 + t, 1), e]
                        dve.scalar_tensor_tensor(xt, ps_d[e % 2][:, t * P:(t + 1) * P], wt, xt,
                                                 ALU.mult, ALU.add).then_inc(x_done, 1)

            turns(dve, body, LAGS, N, E)


def ternary(nc, c, xres, a, out):
    LAGS = 7
    LEVELS = 127.0
    CH = HID // P
    with ExitStack() as ctx:
        m = Mem(nc, ctx, "tern_")
        raw = m.sb("q_raw", [P, 3, HID])
        rounded = m.sb("q_rounded", [P, 3, HID])
        w = m.sb("w_ternary", [P, 3, HID], BF16)
        ones = m.sb("ones", [P, P])
        round_up = m.sb("round_up", [P, 1])
        part = m.sb("part", [P, 3])
        mean = m.sb("mean", [P, 3])
        wscale = m.sb("wscale", [P, 3])
        stats = m.sb("q_stats", [P, 2, 6])
        mean_var = m.sb("q_mean_var", [P, 2, 2])
        var_eps = m.sb("q_var_eps", [P, 2, 1])
        rstd = m.sb("q_rstd", [P, 2, 1])
        z = m.sb("q_z", [P, 2, D])
        size = m.sb("size", [P, 2, 1])
        unit_ = m.sb("unit", [P, 2, 1])
        scale = m.sb("scale", [P, 2, 1])
        back = m.sb("back", [P, UN, 2])
        xr = m.sb("xr", [P, 2, D])
        xq = m.sb("xq", [P, 2, D], BF16)
        xqT = m.sb("xqT", [P, 2, P], BF16)
        gate = m.sb("q_gate", [P, 2, HID])
        hid = m.sb("q_hid", [P, 2, HID])
        hsize = m.sb("hsize", [P, 2, 1])
        hunit = m.sb("hunit", [P, 2, 1])
        hscale = m.sb("hscale", [P, 2, 1])
        hback = m.sb("hback", [P, UN, 1])
        hr = m.sb("hr", [P, 2, HID])
        hq = m.sb("hq", [P, 2, HID], BF16)
        hqT = m.sb("hqT", [P, 2, CH, P], BF16)
        ps_x, ps_h, ps_y, ps_m = (m.ps(n) for n in ("ps_x", "ps_h", "ps_y", "ps_m"))
        ps_g, ps_u = ([m.ps(f"ps_{n}{i}") for i in range(2)] for n in "gu")
        names = ("stats_done", "mv_done", "eps_added", "rstd_done", "z_done", "w_in", "ones_made", "chain", "summed", "w_done", "size_done", "unit_done", "scale_done",
                 "back_done", "xr_done", "xq_done", "x_turned", "xqT_copied", "gu_made", "gate_done", "hid_done",
                 "hsize_done", "hunit_done", "hscale_done", "hback_done", "hr_done", "hq_done", "h_turned",
                 "hqT_copied", "y_made", "x_done")
        (stats_done, mv_done, eps_added, rstd_done, z_done, w_in, ones_made, chain, summed, w_done, size_done, unit_done, scale_done, back_done, xr_done, xq_done,
         x_turned, xqT_copied, gu_made, gate_done, hid_done, hsize_done, hunit_done, hscale_done, hback_done,
         hr_done, hq_done, h_turned, hqT_copied, y_made, x_done) = (m.sem("d_" + n) for n in names)
        x_out = m.sem("d_x_out")
        block = ctx.enter_context(nc.Block())

        @block.sync
        def _(sp):
            for n, name in enumerate(("w_gateT", "w_upT", "w_downT")):
                sp.dma_start(raw[:, n, :], a["L1_ffn_" + name]).then_inc(w_in, 16)
            PARTS = 16
            n = NT // PARTS
            for j in range(PARTS):
                sp.wait_ge(x_done, n * (j + 1))
                sp.dma_start(out[j * n:(j + 1) * n].rearrange("t p d -> p t d"),
                             xres[:, j * n:(j + 1) * n, :]).then_inc(x_out, 16)
            sp.wait_ge(x_out, 16 * PARTS)

        @block.gpsimd
        def _(pool):
            pool.memset(ones[:], 1.0).then_inc(ones_made, 1)
            pool.memset(round_up[:], ROUND).then_inc(ones_made, 1)

            def body(s, k):
                if live(s, 0):
                    b = k % 2
                    pool.wait_ge(eps_added, s + 1)
                    pool.tensor_tensor(rstd[:, b, :], var_eps[:, b, :], c["half_pow"][:, 0:1],
                                       ALU.pow).then_inc(rstd_done, 1)
                if live(s, 1):
                    t, b, kt = s - 1, (k - 1) % 2, (k - 1) % UN
                    pool.wait_ge(unit_done, t + 1)
                    pool.wait_ge(w_done, 1)
                    if since(t, 4):
                        pool.wait_ge(hid_done, t - 3)
                    pool.tensor_tensor(back[:, kt, :], unit_[:, b, :].broadcast_to([P, 2]), mean[:, 0:2],
                                       ALU.mult).then_inc(back_done, 1)
                if live(s, 4):
                    t, b, kt = s - 4, (k - 4) % 2, (k - 4) % UN
                    pool.wait_ge(hunit_done, t + 1)
                    if since(t, 4):
                        pool.wait_ge(x_done, t - 3)
                    pool.tensor_tensor(hback[:, kt, :], hunit[:, b, :], mean[:, 2:3],
                                       ALU.mult).then_inc(hback_done, 1)

            slots(pool, body, LAGS)

        @block.scalar
        def _(act):
            act.wait_ge(ones_made, 2)

            def body(s, k):
                if live(s, 6):
                    t, b = s - 6, (k - 6) % 2
                    act.wait_ge(h_turned, t + 1)
                    if since(t, 2):
                        act.wait_ge(y_made, t - 1)
                    act.copy(hqT[:, b].rearrange("p c n -> p (c n)"),
                             ps_h[:].bitcast(BF16)[:, 0:HID]).then_inc(hqT_copied, 1)
                if live(s, 2):
                    t, b = s - 2, (k - 2) % 2
                    act.wait_ge(x_turned, t + 1)
                    if since(t, 2):
                        act.wait_ge(gu_made, 2 * (t - 1))
                    act.copy(xqT[:, b, :], ps_x[:].bitcast(BF16)[:, 0:P]).then_inc(xqT_copied, 1)
                if live(s, 3):
                    t, b, kt = s - 3, (k - 3) % 2, (k - 3) % UN
                    act.wait_ge(gu_made, 2 * t + 1)
                    act.wait_ge(back_done, t + 1)
                    if since(t, 2):
                        act.wait_ge(hid_done, t - 1)
                    act.activation(gate[:, b], ps_g[b][:], ACT.Silu, scale=back[:, kt, 0:1]).then_inc(gate_done, 1)
                if live(s, 4):
                    t, b = s - 4, (k - 4) % 2
                    act.wait_ge(hscale_done, t + 1)
                    if since(t, 2):
                        act.wait_ge(hq_done, t - 1)
                    act.activation(hr[:, b], hid[:, b], ACT.Identity, bias=round_up[:],
                                   scale=hscale[:, b]).then_inc(hr_done, 1)

            slots(act, body, LAGS)

        @block.tensor
        def _(pe):
            pe.wait_ge(chain, 1)
            pe.wait_ge(ones_made, 2)
            pe.matmul(ps_m[:, 0:3], ones[:], part[:], start=True, stop=True).then_inc(summed, 1)
            pe.wait_ge(w_done, 1)

            def body(s, k):
                if live(s, 3):
                    t, b = s - 3, (k - 3) % 2
                    pe.wait_ge(xqT_copied, t + 1)
                    for i, (out, used) in enumerate(((ps_g[b], gate_done), (ps_u[b], hid_done))):
                        if since(t, 2):
                            pe.wait_ge(used, t - 1)
                        pe.matmul(out[:], xqT[:, b, :], w[:, i, :], start=True, stop=True).then_inc(gu_made, 1)
                if live(s, 2):
                    t, b = s - 2, (k - 2) % 2
                    pe.wait_ge(xq_done, t + 1)
                    if since(t, 1):
                        pe.wait_ge(xqT_copied, t)
                    pe.transpose(ps_x[:].bitcast(BF16)[:, 0:P], xq[:, b, :], c["ident_b"][:]).then_inc(x_turned, 1)
                if live(s, 6):
                    t, b = s - 6, (k - 6) % 2
                    pe.wait_ge(hq_done, t + 1)
                    if since(t, 1):
                        pe.wait_ge(hqT_copied, t)
                    for i in range(CH):
                        mm = pe.transpose(ps_h[:].bitcast(BF16)[:, i * P:(i + 1) * P], hq[:, b, i * P:(i + 1) * P],
                                          c["ident_b"][:])
                    mm.then_inc(h_turned, 1)
                if live(s, 7):
                    t, b = s - 7, (k - 7) % 2
                    pe.wait_ge(hqT_copied, t + 1)
                    if since(t, 1):
                        pe.wait_ge(x_done, t)
                    for i in range(CH):
                        mm = pe.matmul(ps_y[:, 0:P], hqT[:, b, i, :], w[:, 2, i * P:(i + 1) * P],
                                       start=(i == 0), stop=(i == CH - 1))
                    mm.then_inc(y_made, 1)

            slots(pe, body, LAGS)

        @block.vector
        def _(dve):
            dve.wait_ge(w_in, 48)
            dve.tensor_reduce(part[:], raw[:], AX.X, ALU.add, apply_absolute_value=True).then_inc(chain, 1)
            dve.wait_ge(summed, 1)
            dve.tensor_scalar(mean[:], ps_m[:, 0:3], 1.0 / (D * HID), 1e-5, ALU.mult, ALU.max).then_inc(chain, 1)
            dve.wait_ge(chain, 2)
            dve.reciprocal(wscale[:], mean[:]).then_inc(chain, 1)
            dve.wait_ge(chain, 3)
            for n in range(3):
                dve.tensor_scalar(rounded[:, n], raw[:, n], wscale[:, n:n + 1], ROUND,
                                  ALU.mult, ALU.add).then_inc(chain, 1)
            dve.wait_ge(chain, 6)
            dve.tensor_scalar(rounded[:], rounded[:], ROUND, 1.0, ALU.subtract, ALU.min).then_inc(chain, 1)
            dve.wait_ge(chain, 7)
            dve.tensor_scalar(w[:], rounded[:], -1.0, None, ALU.max).then_inc(w_done, 1)
            dve.tensor_scalar(mean[:, 2:3], mean[:, 2:3], c["tanhs"][:, 3:4], None, ALU.mult).then_inc(w_done, 1)

            def body(s, k):
                hid_on, x_on = live(s, 4), live(s, 1)
                t, b, kt = s - 4, (k - 4) % 2, (k - 4) % UN
                n, bn = s - 1, (k - 1) % 2
                if hid_on:
                    dve.wait_ge(gate_done, t + 1)
                    dve.wait_ge(gu_made, 2 * (t + 1))
                    dve.scalar_tensor_tensor(hid[:, b], ps_u[b][:], back[:, kt, 1:2], gate[:, b],
                                             ALU.mult, ALU.mult).then_inc(hid_done, 1)
                if x_on:
                    xt = xres[:, bass.ds(n, 1), :].rearrange("p o d -> p (o d)")
                    dve.wait_ge(rstd_done, n + 1)
                    dve.tensor_scalar(z[:, bn, :], xt, mean_var[:, bn, 0:1], rstd[:, bn, :],
                                      ALU.subtract, ALU.mult).then_inc(z_done, 1)
                if hid_on:
                    dve.wait_ge(hid_done, t + 1)
                    dve.tensor_reduce(hsize[:, b], hid[:, b], AX.X, ALU.max,
                                      apply_absolute_value=True).then_inc(hsize_done, 1)
                if x_on:
                    dve.wait_ge(z_done, n + 1)
                    dve.tensor_reduce(size[:, bn], z[:, bn, :], AX.X, ALU.max,
                                      apply_absolute_value=True).then_inc(size_done, 1)
                if hid_on:
                    dve.wait_ge(hsize_done, t + 1)
                    if since(t, 2):
                        dve.wait_ge(hback_done, t - 1)
                    dve.tensor_scalar(hunit[:, b], hsize[:, b], 1e-5, 1.0 / LEVELS, ALU.max, ALU.mult).then_inc(hunit_done, 1)
                if x_on:
                    dve.wait_ge(size_done, n + 1)
                    if since(n, 2):
                        dve.wait_ge(back_done, n - 1)
                    dve.tensor_scalar(unit_[:, bn], size[:, bn], 1e-5, 1.0 / LEVELS, ALU.max, ALU.mult).then_inc(unit_done, 1)
                if hid_on:
                    dve.wait_ge(hunit_done, t + 1)
                    dve.reciprocal(hscale[:, b], hunit[:, b]).then_inc(hscale_done, 1)
                if x_on:
                    dve.wait_ge(unit_done, n + 1)
                    dve.reciprocal(scale[:, bn], unit_[:, bn]).then_inc(scale_done, 1)
                if x_on:
                    dve.wait_ge(scale_done, n + 1)
                    dve.tensor_scalar(xr[:, bn], z[:, bn, :], scale[:, bn], ROUND, ALU.mult, ALU.add).then_inc(xr_done, 1)
                if live(s, 0):
                    b0 = k % 2
                    dve.bn_stats(stats[:, b0, :], xres[:, bass.ds(s, 1), :]).then_inc(stats_done, 1)
                if live(s, 5):
                    u, bu = s - 5, (k - 5) % 2
                    dve.wait_ge(hr_done, u + 1)
                    if since(u, 2):
                        dve.wait_ge(h_turned, u - 1)
                    dve.tensor_scalar(hq[:, bu], hr[:, bu], ROUND, LEVELS, ALU.subtract, ALU.min).then_inc(hq_done, 1)
                if live(s, 7):
                    o, ko = s - 7, (k - 7) % UN
                    if live(s, 0):
                        dve.wait_ge(stats_done, s + 1)
                    dve.wait_ge(y_made, o + 1)
                    dve.wait_ge(hback_done, o + 1)
                    xt = xres[:, bass.ds(o, 1), :].rearrange("p o d -> p (o d)")
                    dve.scalar_tensor_tensor(xt, ps_y[:, 0:P], hback[:, ko, :], xt, ALU.mult, ALU.add).then_inc(x_done, 1)
                if x_on:
                    dve.wait_ge(xr_done, n + 1)
                    if since(n, 2):
                        dve.wait_ge(x_turned, n - 1)
                    dve.tensor_scalar(xq[:, bn], xr[:, bn], ROUND, LEVELS, ALU.subtract, ALU.min).then_inc(xq_done, 1)
                if live(s, 0):
                    if isinstance(s, int):
                        dve.wait_ge(stats_done, s + 1)
                    dve.bn_aggr(mean_var[:, b0, :], stats[:, b0, :]).then_inc(mv_done, 1)
                    dve.wait_ge(mv_done, s + 1)
                    dve.tensor_scalar(var_eps[:, b0, :], mean_var[:, b0, 1:2], EPS, None,
                                      ALU.add).then_inc(eps_added, 1)

            slots(dve, body, LAGS)


def build(nc, out, a):
    with ExitStack() as ctx:
        m = Mem(nc, ctx)
        xres = m.sb("xres", [P, NT, D])
        c = setup(nc, m, a)
        w_h, w_l = m.sb("w_h", [P, W_ALL], BF16), m.sb("w_l", [P, W_ALL], BF16)
        with ExitStack() as layer0:
            m0 = Mem(nc, layer0)
            zT_h, zT_l = m0.sb("zT_h", [P, NT, P], BF16), m0.sb("zT_l", [P, NT, P], BF16)
            logits = m0.sb("logits", [P, NT, E])
            causal_attention(nc, c, xres, a, zT_h, zT_l, logits, w_h, w_l)
            experts(nc, c, xres, zT_h, zT_l, logits, w_h, w_l)
        perceiver(nc, c, xres, a, w_h, w_l)
        ternary(nc, c, xres, a, out)


def layouts(i):
    import numpy as np

    def chunks(w):
        out, inner = w.shape
        return w.T.reshape(inner // P, P, out).transpose(1, 0, 2).reshape(P, -1)

    a = {"x": i["x"].reshape(NT, P, D), "ctx": i["ctx_1024"].reshape(NT, P, D),
         "mask": i["mask_BxS2_bf1"].view(np.uint8), "g_xattn": i["g_xattn"], "g_ffn": i["g_ffn"]}
    for n in ("wq", "wk", "wv", "wo"):
        a[f"L0_xattn_{n}T"] = i[f"L0_xattn_{n}"].T
    for n in ("bq", "bk", "bv", "bo"):
        a[f"L0_xattn_{n}"] = i[f"L0_xattn_{n}"]
    a["L0_ffn_gate_wT"] = i["L0_ffn_gate_w"].T
    experts = [w.T for n in ("wg", "wu") for w in i[f"L0_ffn_{n}"]] + [chunks(w) for w in i["L0_ffn_wd"]]
    a["split_w"] = np.concatenate(experts + [i["L1_xattn_Wq"], i["L1_xattn_Wkv"]], axis=1)
    for n in ("ln_x_g", "ln_x_b", "ln_l_g", "ln_l_b", "qn_g", "kn_g", "Wout", "bout"):
        a[f"L1_xattn_{n}"] = i[f"L1_xattn_{n}"]
    for n in ("w_gate", "w_up"):
        a[f"L1_ffn_{n}T"] = i[f"L1_ffn_{n}"].T
    a["L1_ffn_w_downT"] = chunks(i["L1_ffn_w_down"])
    return {n: np.ascontiguousarray(v) for n, v in a.items()}


def kernel(**inputs):
    import numpy as np
    import concourse.bacc as bacc
    from concourse.bass_utils import run_bass_kernel_spmd

    nc = bacc.Bacc("TRN2", target_bir_lowering=False, num_devices=1)
    arrays = layouts({n: np.asarray(v) for n, v in inputs.items()})
    a = {n: nc.dram_tensor(n, v.shape, mybir.dt.from_np(v.dtype), kind="ExternalInput").ap()
         for n, v in arrays.items()}
    out = nc.dram_tensor("out", (NT, P, D), F32, kind="ExternalOutput").ap()
    build(nc, out, a)
    r = run_bass_kernel_spmd(nc, [arrays], core_ids=[0])
    return r.results[0]["out"].reshape(B, S, D)
```
